# Optimizing a Trainium2 kernel written in Bass

```python
import numpy as np
import jax
import jax.numpy as jnp

def _softmax(x, axis=-1):
    return jax.nn.softmax(x, axis=axis)

def _gelu(x):
    return jax.nn.gelu(x, approximate=True)

def _silu(x):
    return jax.nn.silu(x)

def _sigmoid(x):
    return jax.nn.sigmoid(x)

def _layernorm(x, axis=-1, eps=1e-05):
    m = jnp.mean(x, axis=axis, keepdims=True)
    v = jnp.var(x, axis=axis, keepdims=True)
    return (x - m) / jnp.sqrt(v + eps)

def _scatter_add(tgt, idx, src, axis=0):
    return tgt.at[idx].add(src)

def _segment_sum(src, seg, n):
    return jax.ops.segment_sum(src, seg, n)
kernel_name = 'mk_seq_preln_d1_jaxref_r8_90b794'

def setup_inputs(seed: int=0):
    np.random.seed(seed)
    _w = jnp.asarray

    def _L0_attn_setup():
        import jax, jax.numpy as jnp
        import numpy as np
        N_HEAD = 16
        PAGE_SIZE = 32
        ROPE_THETA = 10000.0

        def _rope_tables(T, D, dtype):
            inv = 1.0 / ROPE_THETA ** (np.arange(0, D, 2, dtype=np.float32) / D)
            ang = np.outer(np.arange(T, dtype=np.float32), inv)
            return (jnp.asarray(np.cos(ang), dtype), jnp.asarray(np.sin(ang), dtype))

        def _apply_rope(x, cos, sin):
            x1 = x[..., 0::2]
            x2 = x[..., 1::2]
            c = cos[None, :, None, :]
            s = sin[None, :, None, :]
            out = jnp.stack([x1 * c - x2 * s, x1 * s + x2 * c], axis=-1)
            return out.reshape(x.shape)
        key = jax.random.key(seed)
        ks = jax.random.split(key, 6)
        B, T, E = (2, 256, 128)
        L = E // 2
        sc = lambda fan: 1.0 / np.sqrt(fan)
        return {'x': jax.random.normal(ks[0], (B, T, E), jnp.float32), 'wq': jax.random.normal(ks[1], (E, E), jnp.float32) * sc(E), 'w_down': jax.random.normal(ks[2], (E, L), jnp.float32) * sc(E), 'wk_up': jax.random.normal(ks[3], (L, E), jnp.float32) * sc(L), 'wv_up': jax.random.normal(ks[4], (L, E), jnp.float32) * sc(L), 'wo': jax.random.normal(ks[5], (E, E), jnp.float32) * sc(E)}
    _L0_attn_in = _L0_attn_setup()

    def _L0_ffn_setup():
        import jax, jax.numpy as jnp
        import numpy as np
        E = 8
        K = 2
        D = 128
        F = 512
        FS = 256
        B, S = (2, 128)
        key = jax.random.key(seed)
        ks = jax.random.split(key, 8)
        scale = jnp.float32(0.02)
        return {'x': jax.random.normal(ks[0], (B, S, D), jnp.float32), 'gate_w': jax.random.normal(ks[1], (E, D), jnp.float32) * scale, 'gate_k': jax.random.normal(ks[2], (E, D, F), jnp.float32) * scale, 'up_k': jax.random.normal(ks[3], (E, D, F), jnp.float32) * scale, 'down_k': jax.random.normal(ks[4], (E, F, D), jnp.float32) * scale, 'sh_gate': jax.random.normal(ks[5], (D, FS), jnp.float32) * scale, 'sh_up': jax.random.normal(ks[6], (D, FS), jnp.float32) * scale, 'sh_down': jax.random.normal(ks[7], (FS, D), jnp.float32) * scale}
    _L0_ffn_in = _L0_ffn_setup()
    _d = {'L0_attn_x': _L0_attn_in['x'], 'L0_attn_wq': _L0_attn_in['wq'], 'L0_attn_w_down': _L0_attn_in['w_down'], 'L0_attn_wk_up': _L0_attn_in['wk_up'], 'L0_attn_wv_up': _L0_attn_in['wv_up'], 'L0_attn_wo': _L0_attn_in['wo'], 'L0_ffn_gate_w': _L0_ffn_in['gate_w'], 'L0_ffn_gate_k': _L0_ffn_in['gate_k'], 'L0_ffn_up_k': _L0_ffn_in['up_k'], 'L0_ffn_down_k': _L0_ffn_in['down_k'], 'L0_ffn_sh_gate': _L0_ffn_in['sh_gate'], 'L0_ffn_sh_up': _L0_ffn_in['sh_up'], 'L0_ffn_sh_down': _L0_ffn_in['sh_down']}
    _x0 = _d['L0_attn_x']
    _d['L0_attn_x'] = jax.random.normal(jax.random.fold_in(jax.random.key(seed), 1), (4, 1024, 128), dtype=_x0.dtype)
    del _x0
    return _d

def reference(L0_attn_x, L0_attn_wq, L0_attn_w_down, L0_attn_wk_up, L0_attn_wv_up, L0_attn_wo, L0_ffn_gate_w, L0_ffn_gate_k, L0_ffn_up_k, L0_ffn_down_k, L0_ffn_sh_gate, L0_ffn_sh_up, L0_ffn_sh_down):

    def _L0_attn_ref(x, wq, w_down, wk_up, wv_up, wo):
        import jax, jax.numpy as jnp
        import numpy as np
        N_HEAD = 16
        PAGE_SIZE = 32
        ROPE_THETA = 10000.0

        def _rope_tables(T, D, dtype):
            inv = 1.0 / ROPE_THETA ** (np.arange(0, D, 2, dtype=np.float32) / D)
            ang = np.outer(np.arange(T, dtype=np.float32), inv)
            return (jnp.asarray(np.cos(ang), dtype), jnp.asarray(np.sin(ang), dtype))

        def _apply_rope(x, cos, sin):
            x1 = x[..., 0::2]
            x2 = x[..., 1::2]
            c = cos[None, :, None, :]
            s = sin[None, :, None, :]
            out = jnp.stack([x1 * c - x2 * s, x1 * s + x2 * c], axis=-1)
            return out.reshape(x.shape)
        B, T, E = x.shape
        H = N_HEAD
        D = E // H
        q = (x @ wq).reshape(B, T, H, D)
        lat = x @ w_down
        k = (lat @ wk_up).reshape(B, T, H, D)
        v = (lat @ wv_up).reshape(B, T, H, D)
        cos, sin = _rope_tables(T, D, x.dtype)
        q = _apply_rope(q, cos, sin)
        k = _apply_rope(k, cos, sin)
        scale = 1.0 / jnp.sqrt(jnp.asarray(D, x.dtype))
        scores = jnp.einsum('bqhd,bkhd->bhqk', q, k) * scale
        pages = jnp.arange(T) // PAGE_SIZE
        allowed = pages[None, :] <= pages[:, None]
        scores = jnp.where(allowed[None, None], scores, jnp.finfo(scores.dtype).min)
        attn = jax.nn.softmax(scores, axis=-1)
        out = jnp.einsum('bhqk,bkhd->bqhd', attn, v).reshape(B, T, E)
        return out @ wo

    def _L0_ffn_ref(x, gate_w, gate_k, up_k, down_k, sh_gate, sh_up, sh_down):
        import jax, jax.numpy as jnp
        import numpy as np
        E = 8
        K = 2
        D = 128
        F = 512
        FS = 256
        B, S = (2, 128)
        b, s, d = x.shape
        xt = x.reshape(-1, d)
        logits = xt @ gate_w.T
        scores = jax.nn.softmax(logits, axis=-1)
        topk_w, topk_i = jax.lax.top_k(scores, K)
        combine = (jax.nn.one_hot(topk_i, E, dtype=xt.dtype) * topk_w[..., None]).sum(axis=1)
        g = jnp.einsum('nd,edf->enf', xt, gate_k)
        u = jnp.einsum('nd,edf->enf', xt, up_k)
        a = jax.nn.silu(g) * u
        eo = jnp.einsum('enf,efd->end', a, down_k)
        y = jnp.einsum('end,ne->nd', eo, combine)
        shared = jax.nn.silu(xt @ sh_gate) * (xt @ sh_up) @ sh_down
        return (y + shared).reshape(b, s, d)
    x = L0_attn_x
    x = x + _L0_attn_ref(_layernorm(x, axis=-1), L0_attn_wq, L0_attn_w_down, L0_attn_wk_up, L0_attn_wv_up, L0_attn_wo)
    x = x + _L0_ffn_ref(_layernorm(x, axis=-1), L0_ffn_gate_w, L0_ffn_gate_k, L0_ffn_up_k, L0_ffn_down_k, L0_ffn_sh_gate, L0_ffn_sh_up, L0_ffn_sh_down)
    return x

_drawn_inputs = setup_inputs


def setup_inputs(seed=0):
    import zlib

    import numpy as np

    out = dict(_drawn_inputs(seed))
    spreads = {}
    factors = {'L0_ffn_gate_w': 8.0,
     'L0_ffn_gate_k': 8.0,
     'L0_ffn_up_k': 8.0,
     'L0_ffn_down_k': 8.0,
     'L0_ffn_sh_gate': 6.953,
     'L0_ffn_sh_up': 6.86,
     'L0_ffn_sh_down': 6.874}
    for name, (base, spread) in spreads.items():
        noise = np.random.default_rng([zlib.crc32(name.encode()), seed]).standard_normal(out[name].shape)
        drawn = base * np.exp(spread * noise) if base else spread * noise
        out[name] = jnp.asarray(drawn.astype(out[name].dtype))
    for name, factor in factors.items():
        out[name] = (out[name] * factor).astype(out[name].dtype)
    return out
```

```python
from contextlib import ExitStack

import numpy as np

import concourse.bass as bass
from concourse import mybir

F32 = mybir.dt.float32
BF16 = mybir.dt.bfloat16
U32 = mybir.dt.uint32
ALU = mybir.AluOpType
ACT = mybir.ActivationFunctionType
AX = mybir.AxisListType

P = 128
B, T, E = 4, 1024, 128
H, D = 16, 8
HG = 4
GB = H // HG
NG = B * GB
L = 64
PAGE = 32
NPAGE = T // PAGE
W = 512
TC = W // P
NCH = B * T // W
NT = B * T // P
TB = T // P
NE, F, FS = 8, 512, 256
EPS = 1e-5
SCALE = 1.0 / float(np.sqrt(D))
NEG = -1.0e30

Q_SLOTS = ((0, 3), (1, 3), (2, 2))
SLOT_ROWS = 8 * D
MASK_ROW = SLOT_ROWS
MAX_ROW = MASK_ROW + NPAGE
ROWS = MAX_ROW + 3

ROUNDS = [(c, kt) for c in range(T // W) for kt in range(TC * (c + 1))]
NR = len(ROUNDS)


def low(c, t):
    return max(0, P * t - W * c)


def packed(w):
    return 1 if w > W // 2 else W // w


def units_of(w):
    n = packed(w)
    return [list(range(h, h + n)) for h in range(0, HG, n)]


UNITS = [units_of(W - low(c, kt)) for c, kt in ROUNDS]
CUM = [sum(len(u) for u in UNITS[:r]) for r in range(NR + 1)]
NU = CUM[NR]

MAX_SLOTS = [[(0, 3)], [(0, 2)], [(0, 1), (0, 0)], [(0, 4)], [(0, 5)], [(0, 6)], [(0, 7)],
             [(1, 7)], [(1, 6)], [(1, 5), (1, 4)], [], []]


def max_width(ck, qt):
    return min(W, P * (qt + 1) - W * ck)


def max_units():
    n, out = 0, []
    for slot in MAX_SLOTS:
        here = []
        for ck, qt in slot:
            for heads in units_of(max_width(ck, qt)):
                here.append((n, ck, qt, heads))
                n += 1
        out.append(here)
    assert n == NU and n % 2 == 0
    return out


MAX_UNITS = max_units()
MAX_BEFORE = [sum(len(s) for s in MAX_UNITS[:i]) for i in range(NR + 1)]
OT1_SLOT, OT0_SLOT, MT0_SLOT, MT1_SLOT = 1, 5, 6, 11


def build(nc, x, wq, w_down, wk_up, wv_up, wo, gate_w, gate_k, up_k, down_k, sh_gate, sh_up, sh_down,
          cos_t, sin_t, page_k, page_q, eye, iota8, out):
    q_scr = nc.dram_tensor("q_scr", (NG, 3, D * HG, T), BF16).ap()
    k_scr = nc.dram_tensor("k_scr", (NG, 3, D * HG, T), BF16).ap()
    m_scr = nc.dram_tensor("m_scr", (NG, 2, 3, HG * W), BF16).ap()

    with ExitStack() as ctx:
        def sb(name, shape, dt=F32):
            return ctx.enter_context(nc.sbuf_tensor(name, shape, dt))

        def sem(name):
            return ctx.enter_context(nc.semaphore(name))

        ident = sb("ident", [P, P])
        x_all = sb("x_all", [P, NT, E])
        v_all = sb("v_all", [P, NG, TB, HG * (D + 1)])
        attn = sb("attn", [P, NG + 1, TB, HG * D])
        wg_sb = sb("wg_sb", [P, NE, F])
        wu_sb = sb("wu_sb", [P, NE, F])
        wd_sb = sb("wd_sb", [P, NE, F // P, E])
        sg_sb = sb("sg_sb", [P, FS])
        su_sb = sb("su_sb", [P, FS])
        sd_sb = sb("sd_sb", [P, FS // P, E])
        wo_sb = sb("wo_sb", [P, E])
        gw_row = sb("gw_row", [NE, E])
        gw_t = sb("gw_t", [P, NE])
        iota_sb = sb("iota_sb", [P, NE])

        arena = sb("arena", [P, 3 * 2 * HG * T // 2 + 3 * HG * W // 1])
        at = [0]

        def view(words, shape, dt=F32, start=None):
            if start is not None:
                at[0] = start
            v = arena[:, at[0]:at[0] + words]
            at[0] += words
            assert at[0] <= arena.shape[1]
            if dt is not F32:
                v = v.bitcast(dt)
            if len(shape) == 2:
                v = v.rearrange("p (a b) -> p a b", a=shape[0])
            elif len(shape) == 3:
                v = v.rearrange("p (a b c) -> p a b c", a=shape[0], b=shape[1])
            return v

        cos_sb = view(T, (T,), start=0)
        sin_sb = view(T, (T,))
        xn = view(2 * W, (2, W))
        xn_t = view(2 * W, (2, W))
        lat_t = view(2 * W, (2, W))
        rope_a = view(2 * W, (2, W))
        rope_b = view(2 * W, (2, W))
        roped = view(2 * W, (2, W))
        rest = view(2 * W, (2, W))
        parts = view(2 * 3 * W // 2, (2, 3, W), BF16)
        wq_sb = view(E, (E,))
        wq_p = view(E, (E,))
        wq_s = view(E, (E,))
        wk_sb = view(E, (E,))
        wk_p = view(E, (E,))
        wk_s = view(E, (E,))
        wv_sb = view(E, (E,))
        wdn_sb = view(L, (L,))
        QK_WORDS = HG * T // 2
        q_op = [view(QK_WORDS, (HG, T), BF16, start=0 if i == 0 else None) for i in range(3)]
        k_op = [view(QK_WORDS, (HG, T), BF16) for i in range(3)]
        prob = view(3 * HG * W, (3, HG, W))
        a_tok = view(2 * W, (2, W), start=0)
        a_t = view(2 * W, (2, W))
        xn2 = view(2 * W, (2, W))
        xn2_c = view(2 * W, (2, W))
        xn2_t = view(NCH * W, (NCH, W))
        silu = view(2 * W, (2, W))
        act_t = view(2 * W, (2, W))

        v_buf = sb("v_buf", [P, 3, TB, HG * (D + 1)])
        o_sb = sb("o_sb", [P, 2, W])
        o_rec = sb("o_rec", [P, TC * HG])
        mx = sb("mx", [P, 3, HG, TC])
        mx1 = sb("mx1", [P, HG, TC])
        m_neg = sb("m_neg", [HG * TC, 2, P])
        m_rest = sb("m_rest", [HG * TC, 2, P])
        m_part = sb("m_part", [HG * TC, 2, 3, P], BF16)

        st = sb("st", [P, NT, 6])
        mean = sb("mean", [P, NT])
        var = sb("var", [P, NT])
        dif = sb("dif", [P, NT])
        rstd = sb("rstd", [P, NT])
        mv = sb("mv", [P, TC, 2])
        sd4 = sb("sd4", [P, TC])
        rstd4 = sb("rstd4", [P, TC])
        logit = sb("logit", [P, TC, NE])
        top_v = sb("top_v", [P, TC, NE])
        top_i = sb("top_i", [P, TC, NE], U32)
        top_va = sb("top_va", [P, NT, NE])
        top_ia = sb("top_ia", [P, NT, 2])
        e_sum = sb("e_sum", [P, NT])
        top_w = sb("top_w", [P, NT, 2])
        pick = sb("pick", [P, NT, NE])
        comb = sb("comb", [P, NT, NE])

        ps = [ctx.enter_context(nc.psum_tensor(f"ps{i}", [P, W], F32)) for i in range(8)]

        s_x = sem("x_loaded")
        s_w = sem("weights_loaded")
        s_ew = sem("expert_weights_loaded")
        s_vone = sem("v_ones_set")
        s_pc = [sem(f"page_rows_loaded{i}") for i in range(3)]
        s_st = sem("stats_done")
        s_d1 = sem("dve_step")
        s_a1 = sem("act_step")
        s_wp = sem("weights_permuted")
        s_xn = sem("xn_ready")
        s_xtp = sem("xn_turned")
        s_xt = sem("xn_t_ready")
        s_qp = sem("q_projected")
        s_lp = sem("lat_projected")
        s_lt = sem("lat_t_ready")
        s_kp = sem("k_projected")
        s_vp = sem("v_projected")
        s_vr = sem("v_ready")
        s_rm = [sem("rope_q_products"), sem("rope_k_products")]
        s_rs = [sem("q_roped"), sem("k_roped")]
        s_p0 = [sem("q_part0"), sem("k_part0")]
        s_r1 = [sem("q_rest"), sem("k_rest")]
        s_p1 = [sem("q_part1"), sem("k_part1")]
        s_p2 = [sem("q_part2"), sem("k_part2")]
        s_sc = [sem("q_parts_stored"), sem("k_parts_stored")]
        s_ld = [sem(f"qk_loaded{i}") for i in range(3)]
        s_s1 = sem("max_scores")
        s_rd = sem("max_reduced")
        s_m1 = sem("max_joined")
        s_mi = sem("misc_written")
        s_pass = [sem("dve_passed"), sem("pool_passed")]
        s_mn = sem("minus_max")
        s_ms = sem("minus_max_step")
        s_mw = [sem("max_rows_out0"), sem("max_rows_out1")]
        s_mr = [sem("max_rows_in0"), sem("max_rows_in1")]
        s_s2 = sem("scores")
        s_ex = sem("probs")
        s_pv = sem("values_added")
        s_vb = sem("v_buf_ready")
        s_ob = [sem("o_copied0"), sem("o_copied1")]
        s_or = sem("o_reciprocal")
        s_on = sem("attn_ready")
        s_z = sem("zeroed")
        s_at = sem("attn_staged")
        s_atp = sem("attn_turned")
        s_att = sem("attn_t_ready")
        s_y = sem("attn_projected")
        s_x1 = sem("residual_added")
        s_st2 = sem("stats2")
        s_mv = sem("variance2")
        s_sq = sem("deviation2")
        s_rc = sem("rstd2")
        s_xn2 = sem("xn2_ready")
        s_xp2 = sem("xn2_turned")
        s_xc2 = sem("xn2_t_ready")
        s_lg = sem("logits")
        s_lc = sem("logits_copied")
        s_mxv = sem("top_values")
        s_mxi = sem("top_indices")
        s_tk = sem("top_kept")
        s_cx = sem("xn2_t_kept")
        s_gt = sem("gate_w_turned")
        s_gc = sem("gate_w_t_ready")
        s_h = sem("hidden")
        s_si = sem("silu_ready")
        s_ac = sem("act_ready")
        s_dn = sem("down_added")
        s_eo = sem("expert_added")
        s_out = sem("out_stored")

        block = ctx.enter_context(nc.Block())

        x_v = x.rearrange("b (n p) e -> p (b n) e", p=P)
        out_v = out.rearrange("b (n p) e -> p (b n) e", p=P)
        N_LD = 5

        @block.sync
        def _(sp):
            sp.dma_start(x_all[:, 0:NT // 2], x_v[:, 0:NT // 2]).then_inc(s_x, 16)
            sp.dma_start(x_all[:, NT // 2:NT], x_v[:, NT // 2:NT]).then_inc(s_x, 16)
            small = [(ident[:], eye), (wq_sb, wq), (wk_sb[0:L], wk_up), (wv_sb[0:L], wv_up), (wdn_sb, w_down),
                     (cos_sb, cos_t), (sin_sb, sin_t), (wo_sb[:], wo), (gw_row[:], gate_w), (iota_sb[:], iota8)]
            for dst, src in small:
                sp.dma_start(dst, src).then_inc(s_w, 16)
            sp.dma_start(wg_sb[:], gate_k.rearrange("e d f -> d e f")).then_inc(s_ew, 16)
            sp.dma_start(wu_sb[:], up_k.rearrange("e d f -> d e f")).then_inc(s_ew, 16)
            for e in range(NE):
                sp.dma_start(wd_sb[:, e], down_k[e].rearrange("(c p) d -> p c d", p=P)).then_inc(s_ew, 16)
            sp.dma_start(sg_sb[:], sh_gate).then_inc(s_ew, 16)
            sp.dma_start(su_sb[:], sh_up).then_inc(s_ew, 16)
            sp.dma_start(sd_sb[:], sh_down.rearrange("(c p) d -> p c d", p=P)).then_inc(s_ew, 16)

            def store_parts(b, half):
                n = b * 2 + half
                for z, scr in enumerate((q_scr, k_scr)):
                    sp.wait_ge(s_p2[z], n + 1)
                    for g in range(GB):
                        sp.dma_start(scr[b * GB + g, :, :, half * W:half * W + W].rearrange("a r t -> r a t"),
                                     parts[32 * g:32 * g + 32, z]).then_inc(s_sc[z], 16)

            for z in range(2):
                sp.sem_inc(s_sc[z], 1)
            with sp.Fori(0, B) as b:
                for half in range(2):
                    store_parts(b, half)
            for z in range(2):
                sp.wait_ge(s_sc[z], 16 * GB * NCH + 1)

            for i in range(3):
                for dst, src in ((q_op[i], page_q), (k_op[i], page_k)):
                    n = src.shape[0]
                    sp.dma_start(dst[MASK_ROW:MASK_ROW + n],
                                 src.bitcast(BF16).unsqueeze(1).to_broadcast([n, HG, T])).then_inc(s_pc[i], 16)

            def load(i, buf):
                row = 0
                for part, n in Q_SLOTS:
                    src = q_scr[i, part].rearrange("(d j) t -> d (j t)", d=D).unsqueeze(0)
                    sp.dma_start(q_op[buf][row:row + n * D].rearrange("r j t -> r (j t)"),
                                 src.to_broadcast([n, D, HG * T])).then_inc(s_ld[buf], 16)
                    row += n * D
                src = k_scr[i].rearrange("a (d j) t -> (a d) (j t)", d=D)
                sp.dma_start(k_op[buf][0:6 * D].rearrange("r j t -> r (j t)"),
                             src.unsqueeze(0).to_broadcast([2, 3 * D, HG * T])).then_inc(s_ld[buf], 16)
                sp.dma_start(k_op[buf][6 * D:8 * D].rearrange("r j t -> r (j t)"),
                             src[0:2 * D]).then_inc(s_ld[buf], 16)

            def max_rows(i, buf, c):
                sp.wait_ge(s_ms, (i * 2 + c + 1) * 4)
                sp.dma_start(m_scr[i, c].rearrange("a (r n) -> r a n", n=P), m_part[:, c]).then_inc(s_mw[c], 16)
                sp.wait_ge(s_mw[c], (i + 1) * 16)
                sp.dma_start(q_op[buf][MAX_ROW:MAX_ROW + 3, :, c * W:c * W + W],
                             m_scr[i, c].rearrange("a (j t) -> a j t", j=HG)).then_inc(s_mr[c], 16)

            for i in range(3):
                load(i, i)
            for c in range(2):
                max_rows(0, 0, c)

            def group(i, k, more):
                max_rows(i + 1, (k + 1) % 3, 0)
                max_rows(i + 1, (k + 1) % 3, 1)
                if more:
                    sp.wait_ge(s_s2, (i + 1) * NU)
                    load(i + 3, k)

            with sp.Fori(0, 4) as p:
                for k in range(3):
                    group(p * 3 + k, k, True)
            for i in range(12, NG - 1):
                group(i, i % 3, i + 3 < NG)

            with sp.Fori(0, NCH) as n:
                sp.wait_ge(s_eo, (n + 1) * (NE + 1) + 3)
                sp.dma_start(out_v[:, bass.ds(n * TC, TC)], x_all[:, bass.ds(n * TC, TC)]).then_inc(s_out, 16)
            sp.wait_ge(s_out, 16 * NCH)

        @block.gpsimd
        def _(pool):
            def own_wait(s, value):
                pool.wait_ge(s, value)
                pool.sem_inc(s_pass[1], 1)

            pool.memset(v_all[:], 1.0).then_inc(s_vone, 1)

            def project(b, half):
                n = b * 2 + half
                for z in range(2):
                    pool.wait_ge(s_rm[z], n + 1)
                    pool.wait_ge(s_r1[z], n + 1)
                    pool.tensor_tensor(roped[:, z], rope_a[:, z], rope_b[:, z], ALU.add).then_inc(s_rs[z], 1)
                for z in range(2):
                    pool.wait_ge(s_p1[z], n + 1)
                    pool.tensor_tensor(parts[:, z, 2], rest[:, z], parts[:, z, 1],
                                       ALU.subtract).then_inc(s_p2[z], 1)

            with pool.Fori(0, B) as b:
                for half in range(2):
                    project(b, half)

            def values(i, buf):
                pool.tensor_copy(v_buf[:, buf], v_all[:, i]).then_inc(s_vb, 1)

            def split(i, c):
                k = (i * 2 + c) * 4
                own_wait(s_mn, i * 2 + c + 1)
                pool.tensor_copy(m_part[:, c, 0], m_neg[:, c]).then_inc(s_ms, 1)
                pool.wait_ge(s_ms, k + 1)
                pool.tensor_tensor(m_rest[:, c], m_neg[:, c], m_part[:, c, 0], ALU.subtract).then_inc(s_ms, 1)
                own_wait(s_ms, k + 2)
                pool.tensor_copy(m_part[:, c, 1], m_rest[:, c]).then_inc(s_ms, 1)
                pool.wait_ge(s_ms, k + 3)
                pool.tensor_tensor(m_part[:, c, 2], m_rest[:, c], m_part[:, c, 1],
                                   ALU.subtract).then_inc(s_ms, 1)

            pool.wait_ge(s_vr, NCH)
            values(0, 0)
            for c in range(2):
                split(0, c)

            def group(i, k):
                own_wait(s_pv, i * NR + 3)
                values(i + 1, (k + 1) % 3)
                for c in range(2):
                    own_wait(s_mw[c], (i + 1) * 16)
                    split(i + 1, c)

            with pool.Fori(0, (NG - 1) // 3) as p:
                for k in range(3):
                    group(p * 3 + k, k)

            pool.wait_ge(s_on, 2 * NG + 1)
            pool.sem_inc(s_cx, 1)

            def stage(b, half):
                n = b * 2 + half
                own_wait(s_atp, n + 1)
                pool.tensor_copy(a_tok[:, half].rearrange("p (t g e) -> p t g e", t=TC, g=GB),
                                 attn[:, bass.ds(b * GB + 1, GB), half * TC:half * TC + TC]
                                 .rearrange("p g t e -> p t g e")).then_inc(s_at, 1)
            def keep(b, half):
                n = b * 2 + half
                own_wait(s_xc2, n + 1)
                pool.tensor_copy(xn2_t[:, n], xn2_c[:, half]).then_inc(s_cx, 1)

            with pool.Fori(0, B) as b:
                for half in range(2):
                    stage(b, half)
                    keep(b, half)

        @block.scalar
        def _(act):
            act.wait_ge(s_d1, 6)
            act.activation(rstd[:], var[:], ACT.Sqrt).then_inc(s_a1, 1)

            def turn(b, half):
                n = b * 2 + half
                act.wait_ge(s_xtp, n + 1)
                act.activation(xn_t[:, half], ps[0][:], ACT.Copy).then_inc(s_xt, 1)

            def project(b, half, last):
                n = b * 2 + half
                act.wait_ge(s_lp, n + 1)
                act.activation(lat_t[0:L, half], ps[3][0:L], ACT.Copy).then_inc(s_lt, 1)
                if not last:
                    turn(b + (half + 1) // 2, (half + 1) % 2)
                act.wait_ge(s_vp, n + 1)
                for g in range(GB):
                    ins = act.activation(
                        v_all[:, b * GB + g, half * TC:half * TC + TC].rearrange("p t (j e) -> p t j e", j=HG)[:, :, :, 0:D],
                        ps[6][:].rearrange("p (t g j d) -> p t g j d", t=TC, g=GB, j=HG)[:, :, g], ACT.Copy)
                ins.then_inc(s_vr, 1)
                for z in range(2):
                    act.wait_ge(s_rs[z], n + 1)
                    act.wait_ge(s_sc[z], n * 16 * GB + 1)
                    act.activation(parts[:, z, 0], roped[:, z], ACT.Copy).then_inc(s_p0[z], 1)
                for z in range(2):
                    act.wait_ge(s_r1[z], n + 2)
                    act.activation(parts[:, z, 1], rest[:, z], ACT.Copy).then_inc(s_p1[z], 1)

            act.wait_ge(s_vone, 1)
            turn(0, 0)
            with act.Fori(0, B - 1) as b:
                for half in range(2):
                    project(b, half, False)
            for half in range(2):
                project(B - 1, half, half == 1)

            def exps(i, k, r):
                c, kt = ROUNDS[r]
                w = W - low(c, kt)
                for u, heads in enumerate(UNITS[r]):
                    n = CUM[r] + u
                    act.wait_ge(s_s2, i * NU + n + 1)
                    if u == 0:
                        act.wait_ge(s_pv, i * NR + r + 1)
                    act.activation(prob[:, r % 3, heads[0]:heads[0] + len(heads), 0:w],
                                   ps[(NU * k + n) % 3][:, 0:len(heads) * w].rearrange("p (j t) -> p j t", t=w),
                                   ACT.Exp, scale=SCALE).then_inc(s_ex, 1)

            def outputs(i, c):
                act.wait_ge(s_pv, i * NR + (TC if c == 0 else NR) + 3)
                act.activation(o_sb[:, c], ps[5 + c][:], ACT.Copy).then_inc(s_ob[c], 1)

            act.wait_ge(s_z, 2)
            exps(0, 0, 0)

            def group(i, k, last):
                for r in range(NR):
                    if r + 1 < NR:
                        exps(i, k, r + 1)
                    elif not last:
                        exps(i + 1, (k + 1) % 3, 0)
                    if r == 0:
                        outputs(i - 1, 1)
                    if r == TC:
                        outputs(i, 0)

            with act.Fori(0, (NG - 1) // 3) as p:
                for k in range(3):
                    group(p * 3 + k, k, False)
            group(NG - 1, 0, True)
            outputs(NG - 1, 1)

            def project_out(b, half):
                n = b * 2 + half
                act.wait_ge(s_atp, n + 3)
                act.activation(a_t[:, half], ps[0][:], ACT.Copy).then_inc(s_att, 1)
                act.wait_ge(s_mv, n + 1)
                act.activation(sd4[:], mv[:, :, 1], ACT.Sqrt).then_inc(s_sq, 1)
                act.wait_ge(s_xp2, n + 1)
                act.wait_ge(s_cx, n + 1)
                act.activation(xn2_c[:, half], ps[2][:], ACT.Copy).then_inc(s_xc2, 1)

            with act.Fori(0, B) as b:
                for half in range(2):
                    project_out(b, half)

            act.wait_ge(s_d1, 8)
            act.activation(top_va[:], top_va[:], ACT.Exp).then_inc(s_a1, 1)

            NS = NE * (F // P) + FS // P
            with act.Fori(0, NCH) as n:
                for s in range(NS):
                    act.wait_ge(s_h, n * NS + s + 1)
                    act.wait_ge(s_ac, n * NS + s + 1)
                    act.activation(silu[:, s % 2], ps[s % 2][:], ACT.Silu).then_inc(s_si, 1)

        @block.vector
        def _(dve):
            step = [0]

            def chain(ins):
                step[0] += 1
                ins.then_inc(s_d1, 1)
                dve.wait_ge(s_d1, step[0])

            def own_wait(s, value):
                dve.wait_ge(s, value)
                dve.sem_inc(s_pass[0], 1)

            for c in range(2):
                dve.memset(ps[5 + c][:], 1.0).then_inc(s_z, 1)
            dve.sem_inc(s_r1[0], 1)
            dve.sem_inc(s_r1[1], 1)
            dve.sem_inc(s_on, 1)
            dve.sem_inc(s_ac, 2)
            dve.sem_inc(s_eo, 3)
            dve.sem_inc(s_x1, 1)
            dve.sem_inc(s_lc, 1)
            dve.wait_ge(s_x, 32)
            with dve.Fori(0, NT) as t:
                dve.bn_stats(st[:, t], x_all[:, t]).then_inc(s_st, 1)
            dve.wait_ge(s_st, NT)
            chain(dve.tensor_tensor(mean[:], st[:, :, 1], st[:, :, 4], ALU.add))
            chain(dve.tensor_tensor(dif[:], st[:, :, 1], st[:, :, 4], ALU.subtract))
            chain(dve.tensor_tensor(var[:], st[:, :, 2], st[:, :, 5], ALU.add))
            chain(dve.tensor_tensor(dif[:], dif[:], dif[:], ALU.mult))
            chain(dve.tensor_scalar(var[:], var[:], 1.0 / E, EPS, ALU.mult, ALU.add))
            chain(dve.scalar_tensor_tensor(var[:], dif[:], 0.25, var[:], ALU.mult, ALU.add))
            dve.wait_ge(s_a1, 1)
            dve.reciprocal(rstd[:], rstd[:]).then_inc(s_wp, 1)
            dve.tensor_scalar(mean[:], mean[:], 0.5, None, ALU.mult).then_inc(s_wp, 1)

            dve.wait_ge(s_w, 160)
            for full, perm, swap in ((wq_sb, wq_p, wq_s), (wk_sb[0:L], wk_p[0:L], wk_s[0:L])):
                dve.tensor_copy(perm.rearrange("e (g d j) -> e g d j", g=GB, d=D),
                                full.rearrange("e (g j d) -> e g d j", g=GB, d=D)).then_inc(s_wp, 1)
                a = swap.rearrange("e (g i s j) -> e s g i j", g=GB, i=D // 2, s=2)
                b_ = full.rearrange("e (g j i s) -> e s g i j", g=GB, i=D // 2, s=2)
                for s in range(2):
                    for g in range(GB):
                        dve.tensor_copy(a[:, s, g], b_[:, 1 - s, g]).then_inc(s_wp, 1)
            dve.wait_ge(s_wp, 2)

            def normalise(b, half):
                n = b * 2 + half
                for t in range(TC):
                    k = n * TC + t
                    ins = dve.tensor_scalar(xn[:, half, t * P:t * P + P], x_all[:, k],
                                            mean[:, bass.ds(k, 1)], rstd[:, bass.ds(k, 1)],
                                            ALU.subtract, ALU.mult)
                ins.then_inc(s_xn, 1)

            def project(b, half, last):
                n = b * 2 + half
                if not last:
                    normalise(b + (half + 1) // 2, (half + 1) % 2)
                for z, (s_pj, bank) in enumerate(((s_qp, 1), (s_kp, 4))):
                    dve.wait_ge(s_pj, n + 1)
                    dve.tensor_tensor(rope_a[:, z], ps[bank][:], cos_sb[:, half * W:half * W + W], ALU.mult)
                    dve.tensor_tensor(rope_b[:, z], ps[bank + 1][:], sin_sb[:, half * W:half * W + W],
                                      ALU.mult).then_inc(s_rm[z], 1)
                for z in range(2):
                    dve.wait_ge(s_p0[z], n + 1)
                    dve.tensor_tensor(rest[:, z], roped[:, z], parts[:, z, 0], ALU.subtract).then_inc(s_r1[z], 1)

            normalise(0, 0)
            with dve.Fori(0, B - 1) as b:
                for half in range(2):
                    project(b, half, False)
            for half in range(2):
                project(B - 1, half, half == 1)

            def reduce(i, slot):
                for n, ck, qt, heads in MAX_UNITS[slot]:
                    w = max_width(ck, qt)
                    dve.wait_ge(s_s1, i * NU + n + 1)
                    dve.tensor_reduce(mx[:, 0 if qt < TC else 1 + ck, heads[0]:heads[0] + len(heads), qt % TC],
                                      ps[3 + n % 2][:, 0:len(heads) * w].rearrange("p (j t) -> p j t", t=w),
                                      AX.X, ALU.max).then_inc(s_rd, 1)

            def join(i):
                dve.wait_ge(s_rd, (i + 1) * NU)
                dve.tensor_tensor(mx1[:], mx[:, 1], mx[:, 2], ALU.max).then_inc(s_m1, 1)

            def negate(i, c, event):
                dve.wait_ge(s_mi, event + 1)
                dve.tensor_scalar(m_neg[:, c], ps[7][0:HG * TC, 0:P], -1.0, None, ALU.mult).then_inc(s_mn, 1)

            def finish(i, c, place, event):
                dve.wait_ge(s_mi, event + 1)
                o = ps[7][:].rearrange("p (a e) -> p a e", e=32)
                dve.reciprocal(o_rec[:], o[:, :, D]).then_inc(s_or, 1)
                dve.wait_ge(s_or, i * 2 + (1 if c == 1 else 2))
                dve.tensor_tensor(attn[:, place, c * TC:c * TC + TC].rearrange("p t (j d) -> p (t j) d", j=HG),
                                  o[:, :, 0:D], o_rec[:].unsqueeze(2).to_broadcast([P, TC * HG, D]),
                                  ALU.mult).then_inc(s_on, 1)
            for slot in range(NR):
                reduce(0, slot)
            join(0)
            for c in range(2):
                negate(0, c, c)

            def group(i, k, last):
                ev = i * 4 + 2
                for r in range(NR):
                    if not last:
                        reduce(i + 1, r)
                        if r + 1 == MT1_SLOT:
                            join(i + 1)
                    if r == OT1_SLOT:
                        finish(i, 1, i, ev)
                    if r == OT0_SLOT:
                        finish(i, 0, i + 1, ev + 1)
                    if r == MT0_SLOT and not last:
                        dve.wait_ge(s_ms, (i * 2 + 1) * 4)
                        negate(i + 1, 0, ev + 2)
                    if r == MT1_SLOT and not last:
                        dve.wait_ge(s_ms, (i * 2 + 2) * 4)
                        negate(i + 1, 1, ev + 3)

            with dve.Fori(0, (NG - 1) // 3) as p:
                for k in range(3):
                    group(p * 3 + k, k, False)
            group(NG - 1, 0, True)
            finish(NG, 1, NG, 4 * (NG - 1) + 4)

            dve.wait_ge(s_gt, 1)
            dve.tensor_copy(gw_t[:], ps[3][:, 0:NE]).then_inc(s_gc, 1)

            def project_out(b, half):
                n = b * 2 + half
                k = n * TC
                dve.wait_ge(s_y, n + 1)
                dve.tensor_tensor(x_all[:, bass.ds(k, TC)], ps[1][:].rearrange("p (t e) -> p t e", e=E),
                                  x_all[:, bass.ds(k, TC)], ALU.add).then_inc(s_x1, 1)
                own_wait(s_x1, n + 2)
                for t in range(TC):
                    ins = dve.bn_stats(st[:, t], x_all[:, k + t])
                ins.then_inc(s_st2, 1)
                own_wait(s_st2, n + 1)
                for t in range(TC):
                    ins = dve.bn_aggr(mv[:, t], st[:, t])
                ins.then_inc(s_rc, 1)
                dve.wait_ge(s_rc, n * 2 + 1)
                dve.tensor_scalar(mv[:, :, 1], mv[:, :, 1], EPS, None, ALU.add).then_inc(s_mv, 1)
                dve.wait_ge(s_sq, n + 1)
                dve.reciprocal(rstd4[:], sd4[:]).then_inc(s_rc, 1)
                dve.wait_ge(s_rc, n * 2 + 2)
                for t in range(TC):
                    ins = dve.tensor_scalar(xn2[:, half, t * P:t * P + P], x_all[:, k + t],
                                            mv[:, t, 0:1], rstd4[:, t:t + 1], ALU.subtract, ALU.mult)
                ins.then_inc(s_xn2, 1)
                dve.wait_ge(s_lg, n + 1)
                dve.tensor_copy(logit[:], ps[3][:, 0:TC * NE].rearrange("p (t e) -> p t e", e=NE)).then_inc(s_lc, 1)
                own_wait(s_lc, n + 2)
                for t in range(TC):
                    ins = dve.max(top_v[:, t], logit[:, t])
                ins.then_inc(s_mxv, 1)
                own_wait(s_mxv, n + 1)
                for t in range(TC):
                    ins = dve.max_index(top_i[:, t], top_v[:, t], logit[:, t])
                ins.then_inc(s_mxi, 1)
                dve.tensor_copy(top_va[:, bass.ds(k, TC)], top_v[:])
                dve.wait_ge(s_mxi, n + 1)
                dve.tensor_copy(top_ia[:, bass.ds(k, TC)], top_i[:, :, 0:2]).then_inc(s_tk, 1)

            with dve.Fori(0, B) as b:
                for half in range(2):
                    project_out(b, half)
            dve.wait_ge(s_tk, NCH)

            def over(a, n=NE):
                return a.to_broadcast([P, NT, n])

            chain(dve.tensor_copy(e_sum[:], top_va[:, :, 0]))
            chain(dve.tensor_tensor(top_va[:], top_va[:], over(e_sum[:].unsqueeze(2)), ALU.subtract))
            dve.wait_ge(s_a1, 2)
            chain(dve.tensor_reduce(e_sum[:], top_va[:], AX.X, ALU.add))
            chain(dve.reciprocal(e_sum[:], e_sum[:]))
            chain(dve.tensor_tensor(top_w[:], top_va[:, :, 0:2], over(e_sum[:].unsqueeze(2), 2), ALU.mult))
            every = iota_sb[:].unsqueeze(1).to_broadcast([P, NT, NE])
            chain(dve.tensor_tensor(comb[:], every, over(top_ia[:, :, 0:1]), ALU.is_equal))
            chain(dve.tensor_tensor(comb[:], comb[:], over(top_w[:, :, 0:1]), ALU.mult))
            chain(dve.tensor_tensor(pick[:], every, over(top_ia[:, :, 1:2]), ALU.is_equal))
            chain(dve.tensor_tensor(pick[:], pick[:], over(top_w[:, :, 1:2]), ALU.mult))
            chain(dve.tensor_tensor(comb[:], comb[:], pick[:], ALU.add))

            NS = NE * (F // P) + FS // P
            with dve.Fori(0, NCH) as n:
                def add_expert(e):
                    dve.wait_ge(s_dn, n * NS + min(NS, (e + 1) * (F // P)) + 2)
                    dve.wait_ge(s_eo, n * (NE + 1) + e + 3)
                    y = ps[4 + e % 3][:].rearrange("p (t e) -> p t e", e=E)
                    if e < NE:
                        for t in range(TC):
                            k = n * TC + t
                            ins = dve.scalar_tensor_tensor(x_all[:, k], y[:, t], comb[:, k, e:e + 1], x_all[:, k],
                                                           ALU.mult, ALU.add)
                    else:
                        ins = dve.tensor_tensor(x_all[:, bass.ds(n * TC, TC)], y, x_all[:, bass.ds(n * TC, TC)],
                                                ALU.add)
                    ins.then_inc(s_eo, 1)

                for s in range(NS):
                    dve.wait_ge(s_si, n * NS + s + 1)
                    dve.wait_ge(s_dn, n * NS + s + 1)
                    dve.tensor_tensor(act_t[:, s % 2], silu[:, s % 2], ps[2 + s % 2][:], ALU.mult).then_inc(s_ac, 1)
                    if s % 4 == 2 and s > 4:
                        add_expert(s // 4 - 1)
                add_expert(NE - 1)
                add_expert(NE)

        @block.tensor
        def _(pe):
            pe.wait_ge(s_w, 160)

            def turn(b, half):
                n = b * 2 + half
                pe.wait_ge(s_xn, n + 1)
                for t in range(TC):
                    ins = pe.transpose(ps[0][:, t * P:t * P + P], xn[:, half, t * P:t * P + P], ident[:])
                ins.then_inc(s_xtp, 1)

            def project(b, half, last):
                n = b * 2 + half
                pe.wait_ge(s_xt, n + 1)
                pe.wait_ge(s_r1[0], n + 1)
                pe.matmul(ps[1][:], wq_p, xn_t[:, half], start=True, stop=True)
                pe.matmul(ps[2][:], wq_s, xn_t[:, half], start=True, stop=True).then_inc(s_qp, 1)
                pe.matmul(ps[3][0:L], wdn_sb, xn_t[:, half], start=True, stop=True).then_inc(s_lp, 1)
                if not last:
                    turn(b + (half + 1) // 2, (half + 1) % 2)
                pe.wait_ge(s_lt, n + 1)
                pe.wait_ge(s_r1[1], n + 1)
                pe.matmul(ps[4][:], wk_p[0:L], lat_t[0:L, half], start=True, stop=True)
                pe.matmul(ps[5][:], wk_s[0:L], lat_t[0:L, half], start=True, stop=True).then_inc(s_kp, 1)
                for t in range(TC):
                    ins = pe.matmul(ps[6][:, t * P:t * P + P], lat_t[0:L, half, t * P:t * P + P], wv_sb[0:L],
                                    start=True, stop=True)
                ins.then_inc(s_vp, 1)

            pe.wait_ge(s_wp, 20)
            turn(0, 0)
            with pe.Fori(0, B - 1) as b:
                for half in range(2):
                    project(b, half, False)
            for half in range(2):
                project(B - 1, half, half == 1)

            def max_score(i, k, n, ck, qt, heads):
                w = max_width(ck, qt)
                if not (isinstance(i, int) and i == 0 and n < 2):
                    pe.wait_ge(s_rd, i * NU + n - 1)
                for a, j in enumerate(heads):
                    ins = pe.matmul(ps[3 + n % 2][:, a * w:a * w + w], q_op[k][0:MAX_ROW, j, qt * P:qt * P + P],
                                    k_op[k][0:MAX_ROW, j, ck * W:ck * W + w], start=True, stop=True)
                ins.then_inc(s_s1, 1)

            def score(i, k, r, u):
                c, kt = ROUNDS[r]
                lo = low(c, kt)
                w, n = W - lo, CUM[r] + u
                if not (isinstance(i, int) and i == 0 and n < 3):
                    pe.wait_ge(s_ex, i * NU + n - 2)
                for a, j in enumerate(UNITS[r][u]):
                    ins = pe.matmul(ps[(NU * k + n) % 3][:, a * w:a * w + w],
                                    k_op[k][0:ROWS, j, kt * P:kt * P + P],
                                    q_op[k][0:ROWS, j, c * W + lo:c * W + W], start=True, stop=True)
                ins.then_inc(s_s2, 1)

            def add_values(i, k, r):
                c, kt = ROUNDS[r]
                lo = low(c, kt)
                pe.wait_ge(s_ex, i * NU + CUM[r + 1])
                if r == 0:
                    pe.wait_ge(s_vb, i + 1)
                for j in range(HG):
                    ins = pe.matmul(ps[5 + c][32 * j:32 * j + D + 1, lo:W],
                                    v_buf[:, k, kt, j * (D + 1):(j + 1) * (D + 1)], prob[:, r % 3, j, 0:W - lo],
                                    start=(kt == 0), stop=(kt == TC * (c + 1) - 1))
                ins.then_inc(s_pv, 1)

            def turn_max(i, c):
                if c == 0:
                    pe.wait_ge(s_rd, i * NU + MAX_BEFORE[3])
                    src = mx[:, 0].rearrange("p j t -> p (j t)")
                else:
                    pe.wait_ge(s_m1, i + 1)
                    src = mx1[:].rearrange("p j t -> p (j t)")
                pe.transpose(ps[7][0:HG * TC, 0:P], src, ident[:]).then_inc(s_mi, 1)

            def turn_out(c):
                for t in range(TC):
                    ins = pe.transpose(ps[7][:, t * P:t * P + P], o_sb[:, c, t * P:t * P + P], ident[:])
                ins.then_inc(s_mi, 1)

            pe.wait_ge(s_r1[0], NCH + 1)
            pe.wait_ge(s_r1[1], NCH + 1)
            pe.wait_ge(s_vr, NCH)
            pe.wait_ge(s_pc[0], 32)
            pe.wait_ge(s_ld[0], 16 * N_LD)
            for slot in range(NR):
                for n, ck, qt, heads in MAX_UNITS[slot]:
                    max_score(0, 0, n, ck, qt, heads)
            turn_max(0, 0)
            pe.wait_ge(s_mn, 1)
            turn_max(0, 1)
            pe.sem_inc(s_pv, 3)
            pe.wait_ge(s_z, 2)
            pe.wait_ge(s_mr[0], 16)
            for u in range(len(UNITS[0])):
                score(0, 0, 0, u)

            def group(i, k, last):
                nk = (k + 1) % 3
                lap = 16 * N_LD
                for r in range(NR):
                    if r == 0 and not last:
                        pe.wait_ge(s_pc[nk], 32)
                        pe.wait_ge(s_ld[nk], pe_lap(i, k) * lap)
                    si, sk, sr = (i, k, r + 1) if r + 1 < NR else (i + 1, nk, 0)
                    n2 = 0 if (r + 1 == NR and last) else len(UNITS[sr])
                    if n2 and sr in (0, TC):
                        pe.wait_ge(s_mr[0 if sr == 0 else 1], (si + 1) * 16)
                    mine = [] if last else MAX_UNITS[r]
                    for u in range(max(n2, len(mine))):
                        if u < n2:
                            score(si, sk, sr, u)
                        if u < len(mine):
                            max_score(i + 1, nk, *mine[u])
                    add_values(i, k, r)
                    if r == OT1_SLOT:
                        pe.wait_ge(s_ob[1], i + 1)
                        pe.wait_ge(s_mn, i * 2 + 2)
                        turn_out(1)
                    if r == OT0_SLOT:
                        pe.wait_ge(s_ob[0], i + 1)
                        pe.wait_ge(s_on, i * 2 + 2)
                        turn_out(0)
                    if r == MT0_SLOT and not last:
                        pe.wait_ge(s_on, i * 2 + 3)
                        turn_max(i + 1, 0)
                    if r == MT1_SLOT and not last:
                        pe.wait_ge(s_mn, i * 2 + 3)
                        turn_max(i + 1, 1)

            def pe_lap(i, k):
                if isinstance(i, int):
                    return (i + 1) // 3 + 1
                return lap_reg[0] + (1 if k < 2 else 2)

            lap_reg = [None]
            with pe.Fori(0, (NG - 1) // 3) as p:
                lap_reg[0] = p
                for k in range(3):
                    group(p * 3 + k, k, False)
            group(NG - 1, 0, True)
            pe.wait_ge(s_ob[1], NG + 1)
            pe.wait_ge(s_on, 2 * NG + 1)
            turn_out(1)

            pe.wait_ge(s_on, 2 * NG + 2)
            pe.transpose(ps[3][:, 0:NE], gw_row[:], ident[0:NE, 0:NE]).then_inc(s_gt, 1)
            pe.wait_ge(s_gc, 1)
            pe.sem_inc(s_atp, 2)

            def project_out(b, half):
                n = b * 2 + half
                pe.wait_ge(s_at, n + 1)
                for t in range(TC):
                    ins = pe.transpose(ps[0][:, t * P:t * P + P], a_tok[:, half, t * P:t * P + P], ident[:])
                ins.then_inc(s_atp, 1)
                pe.wait_ge(s_att, n + 1)
                pe.wait_ge(s_x1, n + 1)
                for t in range(TC):
                    ins = pe.matmul(ps[1][:, t * P:t * P + P], a_t[:, half, t * P:t * P + P], wo_sb[:],
                                    start=True, stop=True)
                ins.then_inc(s_y, 1)
                pe.wait_ge(s_xn2, n + 1)
                for t in range(TC):
                    ins = pe.transpose(ps[2][:, t * P:t * P + P], xn2[:, half, t * P:t * P + P], ident[:])
                ins.then_inc(s_xp2, 1)
                pe.wait_ge(s_xc2, n + 1)
                pe.wait_ge(s_lc, n + 1)
                for t in range(TC):
                    ins = pe.matmul(ps[3][:, t * NE:t * NE + NE], xn2_c[:, half, t * P:t * P + P], gw_t[:],
                                    start=True, stop=True)
                ins.then_inc(s_lg, 1)

            with pe.Fori(0, B) as b:
                for half in range(2):
                    project_out(b, half)

            slices = [(e, c) for e in range(NE) for c in range(F // P)] + [(NE, c) for c in range(FS // P)]
            NS = len(slices)
            pe.wait_ge(s_ew, 16 * (2 + NE + 3))
            pe.wait_ge(s_cx, NCH + 1)
            pe.wait_ge(s_lc, NCH + 1)
            pe.sem_inc(s_dn, 2)
            with pe.Fori(0, NCH) as n:
                def down(s):
                    e, c = slices[s]
                    last = c == (F // P if e < NE else FS // P) - 1
                    pe.wait_ge(s_ac, n * NS + s + 3)
                    wd = wd_sb[:, e, c] if e < NE else sd_sb[:, c]
                    if c == 0:
                        pe.wait_ge(s_eo, n * (NE + 1) + e + 1)
                    for t in range(TC):
                        ins = pe.matmul(ps[4 + e % 3][:, t * P:t * P + P], act_t[:, s % 2, t * P:t * P + P], wd,
                                        start=(c == 0 and t == 0), stop=last and t == TC - 1,
                                        skip_group_check=True)
                    ins.then_inc(s_dn, 1)

                for s, (e, c) in enumerate(slices):
                    pe.wait_ge(s_ac, n * NS + s + 1)
                    for w_all, w_sh, bank in ((wg_sb, sg_sb, 0), (wu_sb, su_sb, 2)):
                        w = w_all[:, e, c * P:c * P + P] if e < NE else w_sh[:, c * P:c * P + P]
                        ins = pe.matmul(ps[bank + s % 2][:], w, xn2_t[:, n], start=True, stop=True)
                    ins.then_inc(s_h, 1)
                    if s > 0:
                        down(s - 1)
                down(NS - 1)


_INS = ['L0_attn_x', 'L0_attn_wq', 'L0_attn_w_down', 'L0_attn_wk_up', 'L0_attn_wv_up', 'L0_attn_wo',
        'L0_ffn_gate_w', 'L0_ffn_gate_k', 'L0_ffn_up_k', 'L0_ffn_down_k', 'L0_ffn_sh_gate', 'L0_ffn_sh_up',
        'L0_ffn_sh_down']


def shape_tables():
    inv = 1.0 / 10000.0 ** (np.arange(0, D, 2, dtype=np.float32) / D)
    ang = np.outer(np.arange(T, dtype=np.float32), inv)
    cos, sin = np.cos(ang).astype(np.float32), np.sin(ang).astype(np.float32)
    d = (np.arange(P) // HG) % D
    cos_t = cos[:, d // 2].T
    sin_t = sin[:, d // 2].T * np.where(d % 2 == 0, -1.0, 1.0).astype(np.float32)[:, None]
    page = np.arange(T) // PAGE
    rows = np.arange(NPAGE)[:, None]
    page_k = np.concatenate([page[None, :] == rows, np.ones((3, T))])
    page_q = np.where(page[None, :] < rows, NEG, 0.0)
    return {
        "cos_t": np.ascontiguousarray(cos_t, np.float32),
        "sin_t": np.ascontiguousarray(sin_t, np.float32),
        "page_k": (page_k.astype(np.float32).view(np.uint32) >> 16).astype(np.uint16),
        "page_q": (page_q.astype(np.float32).view(np.uint32) >> 16).astype(np.uint16),
        "eye": np.eye(P, dtype=np.float32),
        "iota8": np.tile(np.arange(NE, dtype=np.float32), (P, 1)),
    }


def kernel(**inputs):
    import concourse.bacc as _bacc
    from concourse.bass_utils import run_bass_kernel_spmd as _run

    nc = _bacc.Bacc("TRN2", target_bir_lowering=False, num_devices=1)
    arrays, args = {}, []
    given = [(n, np.ascontiguousarray(inputs[n])) for n in _INS] + list(shape_tables().items())
    for name, a in given:
        arrays[f"in_{name}_dram"] = a
        args.append(nc.dram_tensor(f"in_{name}_dram", a.shape, mybir.dt.from_np(a.dtype), kind="ExternalInput").ap())
    out = nc.dram_tensor("out_0_dram", (B, T, E), F32, kind="ExternalOutput").ap()
    build(nc, *args, out)
    r = _run(nc, [arrays], core_ids=[0])
    return r.results[0]["out_0_dram"]
```

```python
from contextlib import ExitStack

import numpy as np

import concourse.bass as bass
from concourse import mybir

F32 = mybir.dt.float32
BF16 = mybir.dt.bfloat16
U32 = mybir.dt.uint32
I32 = mybir.dt.int32
ALU = mybir.AluOpType
ACT = mybir.ActivationFunctionType
AX = mybir.AxisListType

P = 128
B, T, E = 4, 1024, 128
H, D = 16, 8
HG = 4
GB = H // HG
NG = B * GB
L = 64
PAGE = 32
NPAGE = T // PAGE
W = 512
TC = W // P
NCH = B * T // W
NT = B * T // P
TB = T // P
NE, F, FS = 8, 512, 256
TOP = 2
NBLK = TOP * B * T // P + NE - 1
PLACES = NBLK * P
MAXB = B * T // P
EPS = 1e-5
SCALE = 1.0 / float(np.sqrt(D))
NEG = -1.0e30

Q_SLOTS = ((0, 3), (1, 3), (2, 2))
SLOT_ROWS = 8 * D
MASK_ROW = SLOT_ROWS
MAX_ROW = MASK_ROW + NPAGE
ROWS = MAX_ROW + 3

ROUNDS = [(c, kt) for c in range(T // W) for kt in range(TC * (c + 1))]
NR = len(ROUNDS)


def low(c, t):
    return max(0, P * t - W * c)


def packed(w):
    return 1 if w > W // 2 else W // w


def units_of(w):
    n = packed(w)
    return [list(range(h, h + n)) for h in range(0, HG, n)]


UNITS = [units_of(W - low(c, kt)) for c, kt in ROUNDS]
CUM = [sum(len(u) for u in UNITS[:r]) for r in range(NR + 1)]
NU = CUM[NR]

MAX_SLOTS = [[(0, 3)], [(0, 2)], [(0, 1), (0, 0)], [(0, 4)], [(0, 5)], [(0, 6)], [(0, 7)],
             [(1, 7)], [(1, 6)], [(1, 5), (1, 4)], [], []]


def max_width(ck, qt):
    return min(W, P * (qt + 1) - W * ck)


def max_units():
    n, out = 0, []
    for slot in MAX_SLOTS:
        here = []
        for ck, qt in slot:
            for heads in units_of(max_width(ck, qt)):
                here.append((n, ck, qt, heads))
                n += 1
        out.append(here)
    assert n == NU and n % 2 == 0
    return out


MAX_UNITS = max_units()
MAX_BEFORE = [sum(len(s) for s in MAX_UNITS[:i]) for i in range(NR + 1)]
OT1_SLOT, OT0_SLOT, MT0_SLOT, MT1_SLOT = 1, 5, 6, 11


def build(nc, x, wq, w_down, wk_up, wv_up, wo, gate_w, gate_k, up_k, down_k, sh_gate, sh_up, sh_down,
          cos_t, sin_t, page_k, page_q, eye, before, count_t, out):
    q_scr = nc.dram_tensor("q_scr", (NG, 3, D * HG, T), BF16).ap()
    k_scr = nc.dram_tensor("k_scr", (NG, 3, D * HG, T), BF16).ap()
    x_scr = nc.dram_tensor("x_scr", (PLACES, E), F32).ap()
    y_scr = nc.dram_tensor("y_scr", (PLACES, E), F32).ap()
    m_scr = nc.dram_tensor("m_scr", (NG, 2, 3, HG * W), BF16).ap()

    with ExitStack() as ctx:
        def sb(name, shape, dt=F32):
            return ctx.enter_context(nc.sbuf_tensor(name, shape, dt))

        def sem(name):
            return ctx.enter_context(nc.semaphore(name))

        ident = sb("ident", [P, P])
        x_all = sb("x_all", [P, NT, E])
        v_all = sb("v_all", [P, NG, TB, HG * (D + 1)])
        attn = sb("attn", [P, NG + 1, TB, HG * D])
        wg_sb = sb("wg_sb", [P, NE, F])
        wu_sb = sb("wu_sb", [P, NE, F])
        wd_sb = sb("wd_sb", [P, NE, F // P, E])
        sg_sb = sb("sg_sb", [P, FS])
        su_sb = sb("su_sb", [P, FS])
        sd_sb = sb("sd_sb", [P, FS // P, E])
        wo_sb = sb("wo_sb", [P, E])
        gw_row = sb("gw_row", [NE, E])
        gw_t = sb("gw_t", [P, NE])
        before_sb = sb("before_sb", [P, P])
        ones_sb = sb("ones_sb", [P, P])
        zero_sb = sb("zero_sb", [P, E])
        count_sb = sb("count_sb", [P, NBLK + MAXB])

        arena = sb("arena", [P, 3 * 2 * HG * T // 2 + 3 * HG * W // 1])
        at = [0]

        def view(words, shape, dt=F32, start=None):
            if start is not None:
                at[0] = start
            v = arena[:, at[0]:at[0] + words]
            at[0] += words
            assert at[0] <= arena.shape[1]
            if dt is not F32:
                v = v.bitcast(dt)
            if len(shape) == 2:
                v = v.rearrange("p (a b) -> p a b", a=shape[0])
            elif len(shape) == 3:
                v = v.rearrange("p (a b c) -> p a b c", a=shape[0], b=shape[1])
            return v

        cos_sb = view(T, (T,), start=0)
        sin_sb = view(T, (T,))
        xn = view(2 * W, (2, W))
        xn_t = view(2 * W, (2, W))
        lat_t = view(2 * W, (2, W))
        rope_a = view(2 * W, (2, W))
        rope_b = view(2 * W, (2, W))
        roped = view(2 * W, (2, W))
        rest = view(2 * W, (2, W))
        parts = view(2 * 3 * W // 2, (2, 3, W), BF16)
        wq_sb = view(E, (E,))
        wq_p = view(E, (E,))
        wq_s = view(E, (E,))
        wk_sb = view(E, (E,))
        wk_p = view(E, (E,))
        wk_s = view(E, (E,))
        wv_sb = view(E, (E,))
        wdn_sb = view(L, (L,))
        QK_WORDS = HG * T // 2
        q_op = [view(QK_WORDS, (HG, T), BF16, start=0 if i == 0 else None) for i in range(3)]
        k_op = [view(QK_WORDS, (HG, T), BF16) for i in range(3)]
        prob = view(3 * HG * W, (3, HG, W))
        a_tok = view(2 * W, (2, W), start=0)
        a_t = view(2 * W, (2, W))
        xn2 = view(2 * W, (2, W))
        xn2_c = view(2 * W, (2, W))
        shared_at = at[0]
        xn2_all = view(NT * E, (NT, E))
        xn2_t = view(NCH * W, (NCH, W))
        silu = view(2 * W, (2, W))
        act_t = view(2 * W, (2, W))
        xb = view(2 * E, (2, E))
        xb_t = view(2 * P, (2, P))
        b_silu = view(2 * F, (2, F))
        b_act = view(2 * F, (2, F))
        b_act_t = view(2 * F, (2, F))
        yb = view(2 * E, (2, E))
        y_got = view(TOP * NT * E, (TOP, NT, E), start=shared_at)

        v_buf = sb("v_buf", [P, 3, TB, HG * (D + 1)])
        o_sb = sb("o_sb", [P, 2, W])
        o_rec = sb("o_rec", [P, TC * HG])
        mx = sb("mx", [P, 3, HG, TC])
        mx1 = sb("mx1", [P, HG, TC])
        m_neg = sb("m_neg", [HG * TC, 2, P])
        m_rest = sb("m_rest", [HG * TC, 2, P])
        m_part = sb("m_part", [HG * TC, 2, 3, P], BF16)

        st = sb("st", [P, NT, 6])
        mean = sb("mean", [P, NT])
        var = sb("var", [P, NT])
        dif = sb("dif", [P, NT])
        rstd = sb("rstd", [P, NT])
        logit = sb("logit", [P, TC, NE])
        top_v = sb("top_v", [P, TC, NE])
        top_i = sb("top_i", [P, TC, NE], U32)
        top_va = sb("top_va", [P, NT, NE])
        top_ia = sb("top_ia", [P, NT, 2])
        e_sum = sb("e_sum", [P, NT])
        top_w = sb("top_w", [P, NT, 2])
        pick = [sb(f"pick{i}", [P, NT, NE]) for i in range(TOP)]
        picked = sb("picked", [P, NT, NE])
        total = sb("total", [P, NT, NE])
        upto = [sb(f"upto{i}", [P, NT, NE]) for i in range(2)]
        over_k = sb("over_k", [P, NE, MAXB])
        blocks = sb("blocks", [P, NE])
        b_end = [sb(f"b_end{i}", [P, NE]) for i in range(2)]
        b_base = sb("b_base", [P, NE])
        place = sb("place", [P, NT, NE])
        place_f = [sb(f"place_f{i}", [P, NT]) for i in range(TOP)]
        place_u = [sb(f"place_u{i}", [P, NT], U32) for i in range(TOP)]
        b_past = sb("b_past", [1, NBLK, NE])
        b_exp_f = sb("b_exp_f", [1, NBLK])
        b_exp = sb("b_exp", [1, NBLK], I32)

        ps = [ctx.enter_context(nc.psum_tensor(f"ps{i}", [P, W], F32)) for i in range(8)]

        s_x = sem("x_loaded")
        s_w = sem("weights_loaded")
        s_ew = sem("expert_weights_loaded")
        s_vone = sem("v_ones_set")
        s_pc = [sem(f"page_rows_loaded{i}") for i in range(3)]
        s_st = sem("stats_done")
        s_d1 = sem("dve_step")
        s_a1 = sem("act_step")
        s_wp = sem("weights_permuted")
        s_xn = sem("xn_ready")
        s_xtp = sem("xn_turned")
        s_xt = sem("xn_t_ready")
        s_qp = sem("q_projected")
        s_lp = sem("lat_projected")
        s_lt = sem("lat_t_ready")
        s_kp = sem("k_projected")
        s_vp = sem("v_projected")
        s_vr = sem("v_ready")
        s_rm = [sem("rope_q_products"), sem("rope_k_products")]
        s_rs = [sem("q_roped"), sem("k_roped")]
        s_p0 = [sem("q_part0"), sem("k_part0")]
        s_r1 = [sem("q_rest"), sem("k_rest")]
        s_p1 = [sem("q_part1"), sem("k_part1")]
        s_p2 = [sem("q_part2"), sem("k_part2")]
        s_sc = [sem("q_parts_stored"), sem("k_parts_stored")]
        s_ld = [sem(f"qk_loaded{i}") for i in range(3)]
        s_s1 = sem("max_scores")
        s_rd = sem("max_reduced")
        s_m1 = sem("max_joined")
        s_mi = sem("misc_written")
        s_pass = [sem("dve_passed"), sem("pool_passed")]
        s_mn = sem("minus_max")
        s_ms = sem("minus_max_step")
        s_mw = [sem("max_rows_out0"), sem("max_rows_out1")]
        s_mr = [sem("max_rows_in0"), sem("max_rows_in1")]
        s_s2 = sem("scores")
        s_ex = sem("probs")
        s_pv = sem("values_added")
        s_vb = sem("v_buf_ready")
        s_ob = [sem("o_copied0"), sem("o_copied1")]
        s_or = sem("o_reciprocal")
        s_on = sem("attn_ready")
        s_z = sem("zeroed")
        s_at = sem("attn_staged")
        s_atp = sem("attn_turned")
        s_att = sem("attn_t_ready")
        s_y = sem("attn_projected")
        s_x1 = sem("residual_added")
        s_st2 = sem("stats2")
        s_xn2 = sem("xn2_ready")
        s_xp2 = sem("xn2_turned")
        s_xc2 = sem("xn2_t_ready")
        s_xk2 = sem("xn2_t_kept")
        s_xk = sem("xn2_kept")
        s_lg = sem("logits")
        s_lc = sem("logits_copied")
        s_mxv = sem("top_values")
        s_mxi = sem("top_indices")
        s_tk = sem("top_kept")
        s_gt = sem("gate_w_turned")
        s_gc = sem("gate_w_t_ready")
        s_pk = sem("picked_ready")
        s_cn = sem("picked_counted")
        s_pl = sem("places_ready")
        s_be = sem("block_experts_ready")
        s_h = sem("shared_hidden")
        s_si = sem("shared_silu")
        s_ac = sem("shared_act")
        s_dn = sem("shared_down")
        s_sa = sem("shared_added")
        s_xz = sem("x_scr_cleared")
        s_xs = sem("tokens_scattered")
        s_bl = [sem(f"block_loaded{i}") for i in range(2)]
        s_bx = sem("block_turned")
        s_bt = sem("block_t_ready")
        s_bg = sem("block_gate")
        s_bu = sem("block_up")
        s_bs = sem("block_silu")
        s_ba = sem("block_act")
        s_bp = sem("block_act_turned")
        s_bc = sem("block_act_t_ready")
        s_bd = sem("block_down")
        s_by = sem("block_out_copied")
        s_bo = [sem(f"block_stored{i}") for i in range(2)]
        s_yg = [sem(f"outputs_gathered{n}") for n in range(NCH)]
        s_c1 = sem("first_expert_added")
        s_c2 = sem("second_expert_added")
        s_out = sem("out_stored")

        block = ctx.enter_context(nc.Block())

        x_v = x.rearrange("b (n p) e -> p (b n) e", p=P)
        out_v = out.rearrange("b (n p) e -> p (b n) e", p=P)
        NSH = FS // P
        N_LD = 5

        @block.sync
        def _(sp):
            sp.dma_start(x_all[:, 0:NT // 2], x_v[:, 0:NT // 2]).then_inc(s_x, 16)
            sp.dma_start(x_all[:, NT // 2:NT], x_v[:, NT // 2:NT]).then_inc(s_x, 16)
            small = [(ident[:], eye), (wq_sb, wq), (wk_sb[0:L], wk_up), (wv_sb[0:L], wv_up), (wdn_sb, w_down),
                     (cos_sb, cos_t), (sin_sb, sin_t), (wo_sb[:], wo), (gw_row[:], gate_w), (before_sb[:], before),
                     (count_sb[:], count_t)]
            for dst, src in small:
                sp.dma_start(dst, src).then_inc(s_w, 16)
            sp.dma_start(wg_sb[:], gate_k.rearrange("e d f -> d e f")).then_inc(s_ew, 16)
            sp.dma_start(wu_sb[:], up_k.rearrange("e d f -> d e f")).then_inc(s_ew, 16)
            for e in range(NE):
                sp.dma_start(wd_sb[:, e], down_k[e].rearrange("(c p) d -> p c d", p=P)).then_inc(s_ew, 16)
            sp.dma_start(sg_sb[:], sh_gate).then_inc(s_ew, 16)
            sp.dma_start(su_sb[:], sh_up).then_inc(s_ew, 16)
            sp.dma_start(sd_sb[:], sh_down.rearrange("(c p) d -> p c d", p=P)).then_inc(s_ew, 16)

            sp.wait_ge(s_z, 4)
            sp.dma_start(x_scr.rearrange("(m p) e -> p m e", p=P),
                         zero_sb[:].unsqueeze(1).to_broadcast([P, NBLK, E])).then_inc(s_xz, 16)

            def store_parts(b, half):
                n = b * 2 + half
                for z, scr in enumerate((q_scr, k_scr)):
                    sp.wait_ge(s_p2[z], n + 1)
                    for g in range(GB):
                        sp.dma_start(scr[b * GB + g, :, :, half * W:half * W + W].rearrange("a r t -> r a t"),
                                     parts[32 * g:32 * g + 32, z]).then_inc(s_sc[z], 16)

            for z in range(2):
                sp.sem_inc(s_sc[z], 1)
            with sp.Fori(0, B) as b:
                for half in range(2):
                    store_parts(b, half)
            for z in range(2):
                sp.wait_ge(s_sc[z], 16 * GB * NCH + 1)

            for i in range(3):
                for dst, src in ((q_op[i], page_q), (k_op[i], page_k)):
                    n = src.shape[0]
                    sp.dma_start(dst[MASK_ROW:MASK_ROW + n],
                                 src.bitcast(BF16).unsqueeze(1).to_broadcast([n, HG, T])).then_inc(s_pc[i], 16)

            def load(i, buf):
                row = 0
                for part, n in Q_SLOTS:
                    src = q_scr[i, part].rearrange("(d j) t -> d (j t)", d=D).unsqueeze(0)
                    sp.dma_start(q_op[buf][row:row + n * D].rearrange("r j t -> r (j t)"),
                                 src.to_broadcast([n, D, HG * T])).then_inc(s_ld[buf], 16)
                    row += n * D
                src = k_scr[i].rearrange("a (d j) t -> (a d) (j t)", d=D)
                sp.dma_start(k_op[buf][0:6 * D].rearrange("r j t -> r (j t)"),
                             src.unsqueeze(0).to_broadcast([2, 3 * D, HG * T])).then_inc(s_ld[buf], 16)
                sp.dma_start(k_op[buf][6 * D:8 * D].rearrange("r j t -> r (j t)"),
                             src[0:2 * D]).then_inc(s_ld[buf], 16)

            def max_rows(i, buf, c):
                sp.wait_ge(s_ms, (i * 2 + c + 1) * 4)
                sp.dma_start(m_scr[i, c].rearrange("a (r n) -> r a n", n=P), m_part[:, c]).then_inc(s_mw[c], 16)
                sp.wait_ge(s_mw[c], (i + 1) * 16)
                sp.dma_start(q_op[buf][MAX_ROW:MAX_ROW + 3, :, c * W:c * W + W],
                             m_scr[i, c].rearrange("a (j t) -> a j t", j=HG)).then_inc(s_mr[c], 16)

            for i in range(3):
                load(i, i)
            for c in range(2):
                max_rows(0, 0, c)

            def group(i, k, more):
                max_rows(i + 1, (k + 1) % 3, 0)
                max_rows(i + 1, (k + 1) % 3, 1)
                if more:
                    sp.wait_ge(s_s2, (i + 1) * NU)
                    load(i + 3, k)

            with sp.Fori(0, 4) as p:
                for k in range(3):
                    group(p * 3 + k, k, True)
            for i in range(12, NG - 1):
                group(i, i % 3, i + 3 < NG)

            def block_in(m, par):
                sp.dma_start(xb[:, par], x_scr[bass.ds(m * P, P), :]).then_inc(s_bl[par], 16)

            def block_out(m, par):
                sp.wait_ge(s_by, m + 2)
                sp.dma_start(y_scr[bass.ds(m * P, P), :], yb[:, par]).then_inc(s_bo[par], 16)

            sp.wait_ge(s_xs, 16 * TOP * NT)
            for par in range(2):
                sp.sem_inc(s_bo[par], 1)
                block_in(par, par)

            def slot(m, par):
                sp.wait_ge(s_bx, m + 1)
                block_in(m + 2, par)
                if not (isinstance(m, int) and m < 2):
                    block_out(m - 2, par)

            slot(0, 0)
            slot(1, 1)
            slot(2, 0)
            with sp.Fori(1, (NBLK - 3) // 2) as p:
                for par in (1, 0):
                    slot(p * 2 + (1 if par else 2), par)
            for m in range(NBLK - 4, NBLK):
                block_out(m, m % 2)

            for n in range(NCH):
                sp.wait_ge(s_c2, TC * (n + 1))
                sp.dma_start(out_v[:, n * TC:n * TC + TC], x_all[:, n * TC:n * TC + TC]).then_inc(s_out, 16)
            sp.wait_ge(s_out, 16 * NCH)

        @block.gpsimd
        def _(pool):
            def own_wait(s, value):
                pool.wait_ge(s, value)
                pool.sem_inc(s_pass[1], 1)

            pool.memset(v_all[:], 1.0).then_inc(s_vone, 1)
            pool.memset(ones_sb[:], 1.0).then_inc(s_z, 1)
            pool.memset(zero_sb[:], 0.0).then_inc(s_z, 1)

            def project(b, half):
                n = b * 2 + half
                for z in range(2):
                    pool.wait_ge(s_rm[z], n + 1)
                    pool.wait_ge(s_r1[z], n + 1)
                    pool.tensor_tensor(roped[:, z], rope_a[:, z], rope_b[:, z], ALU.add).then_inc(s_rs[z], 1)
                for z in range(2):
                    pool.wait_ge(s_p1[z], n + 1)
                    pool.tensor_tensor(parts[:, z, 2], rest[:, z], parts[:, z, 1],
                                       ALU.subtract).then_inc(s_p2[z], 1)

            with pool.Fori(0, B) as b:
                for half in range(2):
                    project(b, half)

            def values(i, buf):
                pool.tensor_copy(v_buf[:, buf], v_all[:, i]).then_inc(s_vb, 1)

            def split(i, c):
                k = (i * 2 + c) * 4
                own_wait(s_mn, i * 2 + c + 1)
                pool.tensor_copy(m_part[:, c, 0], m_neg[:, c]).then_inc(s_ms, 1)
                pool.wait_ge(s_ms, k + 1)
                pool.tensor_tensor(m_rest[:, c], m_neg[:, c], m_part[:, c, 0], ALU.subtract).then_inc(s_ms, 1)
                own_wait(s_ms, k + 2)
                pool.tensor_copy(m_part[:, c, 1], m_rest[:, c]).then_inc(s_ms, 1)
                pool.wait_ge(s_ms, k + 3)
                pool.tensor_tensor(m_part[:, c, 2], m_rest[:, c], m_part[:, c, 1],
                                   ALU.subtract).then_inc(s_ms, 1)

            pool.wait_ge(s_vr, NCH)
            values(0, 0)
            for c in range(2):
                split(0, c)

            def group(i, k):
                own_wait(s_pv, i * NR + 3)
                values(i + 1, (k + 1) % 3)
                for c in range(2):
                    own_wait(s_mw[c], (i + 1) * 16)
                    split(i + 1, c)

            with pool.Fori(0, (NG - 1) // 3) as p:
                for k in range(3):
                    group(p * 3 + k, k)

            pool.wait_ge(s_on, 2 * NG + 1)

            def stage(b, half):
                n = b * 2 + half
                own_wait(s_atp, n + 1)
                pool.tensor_copy(a_tok[:, half].rearrange("p (t g e) -> p t g e", t=TC, g=GB),
                                 attn[:, bass.ds(b * GB + 1, GB), half * TC:half * TC + TC]
                                 .rearrange("p g t e -> p t g e")).then_inc(s_at, 1)

            with pool.Fori(0, B) as b:
                for half in range(2):
                    stage(b, half)

            with pool.Fori(0, B) as b:
                for half in range(2):
                    own_wait(s_xn2, b * 2 + half + 1)
                    pool.tensor_copy(xn2_all[:, bass.ds((b * 2 + half) * TC, TC)],
                                     xn2[:, half].rearrange("p (t e) -> p t e", e=E)).then_inc(s_xk, 1)

            pool.wait_ge(s_xk, NCH)
            pool.wait_ge(s_pl, 2)
            pool.wait_ge(s_xz, 16)
            for t in range(NT):
                for i in range(TOP):
                    pool.indirect_dma_start(x_scr, bass.IndirectOffsetOnAxis(ap=place_u[i][:, t:t + 1], axis=0),
                                            xn2_all[:, t], None, bounds_check=PLACES - 1).then_inc(s_xs, 16)

            for par in range(2):
                pool.wait_ge(s_bo[par], 16 * ((NBLK + 1 - par) // 2) + 1)
            for t in range(NT):
                for i in range(TOP):
                    pool.indirect_dma_start(y_got[:, i, t], None, y_scr,
                                            bass.IndirectOffsetOnAxis(ap=place_u[i][:, t:t + 1], axis=0),
                                            bounds_check=PLACES - 1).then_inc(s_yg[t // TC], 16)

        @block.scalar
        def _(act):
            act.wait_ge(s_d1, 6)
            act.activation(rstd[:], var[:], ACT.Sqrt).then_inc(s_a1, 1)

            def turn(b, half):
                n = b * 2 + half
                act.wait_ge(s_xtp, n + 1)
                act.activation(xn_t[:, half], ps[0][:], ACT.Copy).then_inc(s_xt, 1)

            def project(b, half, last):
                n = b * 2 + half
                act.wait_ge(s_lp, n + 1)
                act.activation(lat_t[0:L, half], ps[3][0:L], ACT.Copy).then_inc(s_lt, 1)
                if not last:
                    turn(b + (half + 1) // 2, (half + 1) % 2)
                act.wait_ge(s_vp, n + 1)
                for g in range(GB):
                    ins = act.activation(
                        v_all[:, b * GB + g, half * TC:half * TC + TC].rearrange("p t (j e) -> p t j e", j=HG)[:, :, :, 0:D],
                        ps[6][:].rearrange("p (t g j d) -> p t g j d", t=TC, g=GB, j=HG)[:, :, g], ACT.Copy)
                ins.then_inc(s_vr, 1)
                for z in range(2):
                    act.wait_ge(s_rs[z], n + 1)
                    act.wait_ge(s_sc[z], n * 16 * GB + 1)
                    act.activation(parts[:, z, 0], roped[:, z], ACT.Copy).then_inc(s_p0[z], 1)
                for z in range(2):
                    act.wait_ge(s_r1[z], n + 2)
                    act.activation(parts[:, z, 1], rest[:, z], ACT.Copy).then_inc(s_p1[z], 1)

            act.wait_ge(s_vone, 1)
            turn(0, 0)
            with act.Fori(0, B - 1) as b:
                for half in range(2):
                    project(b, half, False)
            for half in range(2):
                project(B - 1, half, half == 1)

            def exps(i, k, r):
                c, kt = ROUNDS[r]
                w = W - low(c, kt)
                for u, heads in enumerate(UNITS[r]):
                    n = CUM[r] + u
                    act.wait_ge(s_s2, i * NU + n + 1)
                    if u == 0:
                        act.wait_ge(s_pv, i * NR + r + 1)
                    act.activation(prob[:, r % 3, heads[0]:heads[0] + len(heads), 0:w],
                                   ps[(NU * k + n) % 3][:, 0:len(heads) * w].rearrange("p (j t) -> p j t", t=w),
                                   ACT.Exp, scale=SCALE).then_inc(s_ex, 1)

            def outputs(i, c):
                act.wait_ge(s_pv, i * NR + (TC if c == 0 else NR) + 3)
                act.activation(o_sb[:, c], ps[5 + c][:], ACT.Copy).then_inc(s_ob[c], 1)

            act.wait_ge(s_z, 4)
            exps(0, 0, 0)

            def group(i, k, last):
                for r in range(NR):
                    if r + 1 < NR:
                        exps(i, k, r + 1)
                    elif not last:
                        exps(i + 1, (k + 1) % 3, 0)
                    if r == 0:
                        outputs(i - 1, 1)
                    if r == TC:
                        outputs(i, 0)

            with act.Fori(0, (NG - 1) // 3) as p:
                for k in range(3):
                    group(p * 3 + k, k, False)
            group(NG - 1, 0, True)
            outputs(NG - 1, 1)

            def project_out(b, half):
                n = b * 2 + half
                act.wait_ge(s_atp, n + 3)
                act.activation(a_t[:, half], ps[0][:], ACT.Copy).then_inc(s_att, 1)

            with act.Fori(0, B) as b:
                for half in range(2):
                    project_out(b, half)
            act.wait_ge(s_d1, 14)
            act.activation(rstd[:], var[:], ACT.Sqrt).then_inc(s_a1, 1)

            def keep(b, half):
                n = b * 2 + half
                act.wait_ge(s_xp2, n + 1)
                act.activation(xn2_c[:, half], ps[2][:], ACT.Copy).then_inc(s_xc2, 1)
                act.activation(xn2_t[:, n], ps[2][:], ACT.Copy).then_inc(s_xk2, 1)

            with act.Fori(0, B) as b:
                for half in range(2):
                    keep(b, half)

            act.wait_ge(s_d1, 18)
            act.activation(top_va[:], top_va[:], ACT.Exp).then_inc(s_a1, 1)

            with act.Fori(0, NCH) as n:
                for s in range(NSH):
                    act.wait_ge(s_h, n * NSH + s + 1)
                    act.wait_ge(s_ac, n * NSH + s + 1)
                    act.activation(silu[:, s % 2], ps[s % 2][:], ACT.Silu).then_inc(s_si, 1)

            def block_t(m, par):
                act.wait_ge(s_bx, m + 1)
                act.activation(xb_t[:, par], ps[0][:, 0:P], ACT.Copy).then_inc(s_bt, 1)

            def block_silu(m, par):
                act.wait_ge(s_bg, m + 1)
                if not (isinstance(m, int) and m < 2):
                    act.wait_ge(s_ba, m - 1)
                act.activation(b_silu[:, par], ps[1 + par][:], ACT.Silu).then_inc(s_bs, 1)

            def block_y(m, par, lap):
                act.wait_ge(s_bd, m + 1)
                act.wait_ge(s_bo[par], lap * 16 + 1)
                act.activation(yb[:, par], ps[7][:, 0:E], ACT.Copy).then_inc(s_by, 1)

            def slot(m, par, lap):
                block_silu(m, par)
                if not (isinstance(m, int) and m < 2):
                    block_y(m - 2, par, lap - 1)
                if not (isinstance(m, int) and m + 1 >= NBLK):
                    block_t(m + 1, 1 - par)

            act.sem_inc(s_by, 1)
            block_t(0, 0)
            for m in range(2):
                slot(m, m, 0)
            with act.Fori(1, NBLK // 2) as p:
                for par in range(2):
                    slot(p * 2 + par, par, p)
            slot(NBLK - 1, 0, NBLK // 2)
            block_y(NBLK - 2, 1, (NBLK - 2) // 2)
            block_y(NBLK - 1, 0, (NBLK - 1) // 2)

        @block.vector
        def _(dve):
            step = [0]

            def chain(ins):
                step[0] += 1
                ins.then_inc(s_d1, 1)
                dve.wait_ge(s_d1, step[0])

            def own_wait(s, value):
                dve.wait_ge(s, value)
                dve.sem_inc(s_pass[0], 1)

            for c in range(2):
                dve.memset(ps[5 + c][:], 1.0).then_inc(s_z, 1)
            dve.sem_inc(s_r1[0], 1)
            dve.sem_inc(s_r1[1], 1)
            dve.sem_inc(s_on, 1)
            dve.sem_inc(s_ac, 2)
            dve.sem_inc(s_sa, 1)
            dve.sem_inc(s_x1, 1)
            dve.sem_inc(s_lc, 1)
            dve.wait_ge(s_x, 32)
            with dve.Fori(0, NT) as t:
                dve.bn_stats(st[:, t], x_all[:, t]).then_inc(s_st, 1)
            dve.wait_ge(s_st, NT)

            def moments(turn):
                chain(dve.tensor_tensor(mean[:], st[:, :, 1], st[:, :, 4], ALU.add))
                chain(dve.tensor_tensor(dif[:], st[:, :, 1], st[:, :, 4], ALU.subtract))
                chain(dve.tensor_tensor(var[:], st[:, :, 2], st[:, :, 5], ALU.add))
                chain(dve.tensor_tensor(dif[:], dif[:], dif[:], ALU.mult))
                chain(dve.tensor_scalar(var[:], var[:], 1.0 / E, EPS, ALU.mult, ALU.add))
                chain(dve.scalar_tensor_tensor(var[:], dif[:], 0.25, var[:], ALU.mult, ALU.add))
                dve.wait_ge(s_a1, turn)
                chain(dve.reciprocal(rstd[:], rstd[:]))
                chain(dve.tensor_scalar(mean[:], mean[:], 0.5, None, ALU.mult))

            moments(1)

            dve.wait_ge(s_w, 16 * 11)
            for full, perm, swap in ((wq_sb, wq_p, wq_s), (wk_sb[0:L], wk_p[0:L], wk_s[0:L])):
                dve.tensor_copy(perm.rearrange("e (g d j) -> e g d j", g=GB, d=D),
                                full.rearrange("e (g j d) -> e g d j", g=GB, d=D)).then_inc(s_wp, 1)
                a = swap.rearrange("e (g i s j) -> e s g i j", g=GB, i=D // 2, s=2)
                b_ = full.rearrange("e (g j i s) -> e s g i j", g=GB, i=D // 2, s=2)
                for s in range(2):
                    for g in range(GB):
                        dve.tensor_copy(a[:, s, g], b_[:, 1 - s, g]).then_inc(s_wp, 1)

            def normalise(b, half):
                n = b * 2 + half
                for t in range(TC):
                    k = n * TC + t
                    ins = dve.tensor_scalar(xn[:, half, t * P:t * P + P], x_all[:, k],
                                            mean[:, bass.ds(k, 1)], rstd[:, bass.ds(k, 1)],
                                            ALU.subtract, ALU.mult)
                ins.then_inc(s_xn, 1)

            def project(b, half, last):
                n = b * 2 + half
                if not last:
                    normalise(b + (half + 1) // 2, (half + 1) % 2)
                for z, (s_pj, bank) in enumerate(((s_qp, 1), (s_kp, 4))):
                    dve.wait_ge(s_pj, n + 1)
                    dve.tensor_tensor(rope_a[:, z], ps[bank][:], cos_sb[:, half * W:half * W + W], ALU.mult)
                    dve.tensor_tensor(rope_b[:, z], ps[bank + 1][:], sin_sb[:, half * W:half * W + W],
                                      ALU.mult).then_inc(s_rm[z], 1)
                for z in range(2):
                    dve.wait_ge(s_p0[z], n + 1)
                    dve.tensor_tensor(rest[:, z], roped[:, z], parts[:, z, 0], ALU.subtract).then_inc(s_r1[z], 1)

            normalise(0, 0)
            with dve.Fori(0, B - 1) as b:
                for half in range(2):
                    project(b, half, False)
            for half in range(2):
                project(B - 1, half, half == 1)

            def reduce(i, slot):
                for n, ck, qt, heads in MAX_UNITS[slot]:
                    w = max_width(ck, qt)
                    dve.wait_ge(s_s1, i * NU + n + 1)
                    dve.tensor_reduce(mx[:, 0 if qt < TC else 1 + ck, heads[0]:heads[0] + len(heads), qt % TC],
                                      ps[3 + n % 2][:, 0:len(heads) * w].rearrange("p (j t) -> p j t", t=w),
                                      AX.X, ALU.max).then_inc(s_rd, 1)

            def join(i):
                dve.wait_ge(s_rd, (i + 1) * NU)
                dve.tensor_tensor(mx1[:], mx[:, 1], mx[:, 2], ALU.max).then_inc(s_m1, 1)

            def negate(i, c, event):
                dve.wait_ge(s_mi, event + 1)
                dve.tensor_scalar(m_neg[:, c], ps[7][0:HG * TC, 0:P], -1.0, None, ALU.mult).then_inc(s_mn, 1)

            def finish(i, c, place, event):
                dve.wait_ge(s_mi, event + 1)
                o = ps[7][:].rearrange("p (a e) -> p a e", e=32)
                dve.reciprocal(o_rec[:], o[:, :, D]).then_inc(s_or, 1)
                dve.wait_ge(s_or, i * 2 + (1 if c == 1 else 2))
                dve.tensor_tensor(attn[:, place, c * TC:c * TC + TC].rearrange("p t (j d) -> p (t j) d", j=HG),
                                  o[:, :, 0:D], o_rec[:].unsqueeze(2).to_broadcast([P, TC * HG, D]),
                                  ALU.mult).then_inc(s_on, 1)
            for slot in range(NR):
                reduce(0, slot)
            join(0)
            for c in range(2):
                negate(0, c, c)

            def group(i, k, last):
                ev = i * 4 + 2
                for r in range(NR):
                    if not last:
                        reduce(i + 1, r)
                        if r + 1 == MT1_SLOT:
                            join(i + 1)
                    if r == OT1_SLOT:
                        finish(i, 1, i, ev)
                    if r == OT0_SLOT:
                        finish(i, 0, i + 1, ev + 1)
                    if r == MT0_SLOT and not last:
                        dve.wait_ge(s_ms, (i * 2 + 1) * 4)
                        negate(i + 1, 0, ev + 2)
                    if r == MT1_SLOT and not last:
                        dve.wait_ge(s_ms, (i * 2 + 2) * 4)
                        negate(i + 1, 1, ev + 3)

            with dve.Fori(0, (NG - 1) // 3) as p:
                for k in range(3):
                    group(p * 3 + k, k, False)
            group(NG - 1, 0, True)
            finish(NG, 1, NG, 4 * (NG - 1) + 4)

            dve.wait_ge(s_gt, 1)
            dve.tensor_copy(gw_t[:], ps[3][:, 0:NE]).then_inc(s_gc, 1)

            def project_out(b, half):
                n = b * 2 + half
                k = n * TC
                dve.wait_ge(s_y, n + 1)
                dve.tensor_tensor(x_all[:, bass.ds(k, TC)], ps[1][:].rearrange("p (t e) -> p t e", e=E),
                                  x_all[:, bass.ds(k, TC)], ALU.add).then_inc(s_x1, 1)
                own_wait(s_x1, n + 2)
                for t in range(TC):
                    ins = dve.bn_stats(st[:, k + t], x_all[:, k + t])
                ins.then_inc(s_st2, 1)

            with dve.Fori(0, B) as b:
                for half in range(2):
                    project_out(b, half)
            dve.wait_ge(s_st2, NCH)
            moments(2)

            def choose(b, half):
                n = b * 2 + half
                k = n * TC
                if not isinstance(b, int) or n > 1:
                    dve.wait_ge(s_xk, n - 1)
                    dve.wait_ge(s_xp2, n - 1)
                for t in range(TC):
                    ins = dve.tensor_scalar(xn2[:, half, t * P:t * P + P], x_all[:, k + t],
                                            mean[:, bass.ds(k + t, 1)], rstd[:, bass.ds(k + t, 1)],
                                            ALU.subtract, ALU.mult)
                ins.then_inc(s_xn2, 1)

            def top(b, half):
                n = b * 2 + half
                k = n * TC
                dve.wait_ge(s_lg, n + 1)
                dve.tensor_copy(logit[:], ps[3][:, 0:TC * NE].rearrange("p (t e) -> p t e", e=NE)).then_inc(s_lc, 1)
                own_wait(s_lc, n + 2)
                for t in range(TC):
                    ins = dve.max(top_v[:, t], logit[:, t])
                ins.then_inc(s_mxv, 1)
                own_wait(s_mxv, n + 1)
                for t in range(TC):
                    ins = dve.max_index(top_i[:, t], top_v[:, t], logit[:, t])
                ins.then_inc(s_mxi, 1)
                dve.tensor_copy(top_va[:, bass.ds(k, TC)], top_v[:])
                dve.wait_ge(s_mxi, n + 1)
                dve.tensor_copy(top_ia[:, bass.ds(k, TC)], top_i[:, :, 0:2]).then_inc(s_tk, 1)

            choose(0, 0)
            choose(0, 1)
            with dve.Fori(0, B - 1) as b:
                for half in range(2):
                    choose(b + 1, half)
                    top(b, half)
            top(B - 1, 0)
            top(B - 1, 1)
            dve.wait_ge(s_tk, NCH)

            def over(a, n=NE):
                return a.to_broadcast([P, NT, n])

            chain(dve.tensor_copy(e_sum[:], top_va[:, :, 0]))
            chain(dve.tensor_tensor(top_va[:], top_va[:], over(e_sum[:].unsqueeze(2)), ALU.subtract))
            every = count_sb[:, 0:NE].unsqueeze(1).to_broadcast([P, NT, NE])
            for i in range(TOP):
                chain(dve.tensor_tensor(pick[i][:], every, over(top_ia[:, :, i:i + 1]), ALU.is_equal))
            dve.tensor_tensor(picked[:], pick[0][:], pick[1][:], ALU.add).then_inc(s_pk, 1)
            dve.wait_ge(s_a1, 3)
            chain(dve.tensor_reduce(e_sum[:], top_va[:], AX.X, ALU.add))
            chain(dve.reciprocal(e_sum[:], e_sum[:]))
            chain(dve.tensor_tensor(top_w[:], top_va[:, :, 0:2], over(e_sum[:].unsqueeze(2), 2), ALU.mult))

            dve.wait_ge(s_cn, 1)
            chain(dve.tensor_copy(total[:], ps[5][:, 0:NT * NE].rearrange("p (t e) -> p t e", e=NE)))
            a, z, k = total, 0, 1
            while k < NT:
                chain(dve.tensor_tensor(upto[z][:, k:NT], a[:, k:NT], a[:, 0:NT - k], ALU.add))
                chain(dve.tensor_copy(upto[z][:, 0:k], a[:, 0:k]))
                a, z, k = upto[z], 1 - z, 2 * k
            chain(dve.tensor_tensor(over_k[:], a[:, NT - 1].unsqueeze(2).to_broadcast([P, NE, MAXB]),
                                    count_sb[:, NBLK:NBLK + MAXB].unsqueeze(1).to_broadcast([P, NE, MAXB]),
                                    ALU.is_gt))
            chain(dve.tensor_reduce(blocks[:], over_k[:], AX.X, ALU.add))
            c, k, y = blocks, 1, 0
            while k < NE:
                chain(dve.tensor_tensor(b_end[y][:, k:NE], c[:, k:NE], c[:, 0:NE - k], ALU.add))
                chain(dve.tensor_copy(b_end[y][:, 0:k], c[:, 0:k]))
                c, k, y = b_end[y], 2 * k, 1 - y
            chain(dve.tensor_tensor(b_base[:], c[:], blocks[:], ALU.subtract))
            chain(dve.tensor_scalar(b_base[:], b_base[:], float(P), None, ALU.mult))
            chain(dve.tensor_tensor(place[:], a[:], total[:], ALU.subtract))
            chain(dve.tensor_tensor(place[:], place[:], b_base[:].unsqueeze(1).to_broadcast([P, NT, NE]), ALU.add))
            chain(dve.tensor_tensor(place[:], ps[4][:, 0:NT * NE].rearrange("p (t e) -> p t e", e=NE), place[:],
                                    ALU.add))
            for i in range(TOP):
                chain(dve.tensor_tensor(pick[i][:], pick[i][:], place[:], ALU.mult))
                chain(dve.tensor_reduce(place_f[i][:], pick[i][:], AX.X, ALU.add))
                dve.tensor_copy(place_u[i][:], place_f[i][:]).then_inc(s_pl, 1)
            chain(dve.tensor_tensor(b_past[:], c[0:1].unsqueeze(1).to_broadcast([1, NBLK, NE]),
                                    count_sb[0:1, 0:NBLK].unsqueeze(2).to_broadcast([1, NBLK, NE]), ALU.is_le))
            chain(dve.tensor_reduce(b_exp_f[:], b_past[:], AX.X, ALU.add))
            dve.tensor_scalar(b_exp[:], b_exp_f[:], float(NE - 1), None, ALU.min).then_inc(s_be, 1)

            with dve.Fori(0, NCH) as n:
                for s in range(NSH):
                    dve.wait_ge(s_si, n * NSH + s + 1)
                    dve.wait_ge(s_dn, n * NSH + s + 1)
                    dve.tensor_tensor(act_t[:, s % 2], silu[:, s % 2], ps[2 + s % 2][:], ALU.mult).then_inc(s_ac, 1)
                dve.wait_ge(s_dn, n * NSH + NSH + 2)
                dve.tensor_tensor(x_all[:, bass.ds(n * TC, TC)], ps[6][:].rearrange("p (t e) -> p t e", e=E),
                                  x_all[:, bass.ds(n * TC, TC)], ALU.add).then_inc(s_sa, 1)

            def block_act(m, par):
                dve.wait_ge(s_bs, m + 1)
                dve.wait_ge(s_bu, m + 1)
                dve.tensor_tensor(b_act[:, par], b_silu[:, par], ps[3 + par][:], ALU.mult).then_inc(s_ba, 1)

            def block_act_t(m, par):
                dve.wait_ge(s_bp, m + 1)
                dve.tensor_copy(b_act_t[:, par], ps[5 + par][:]).then_inc(s_bc, 1)

            def slot(m, par):
                block_act(m, par)
                if not (isinstance(m, int) and m < 1):
                    block_act_t(m - 1, 1 - par)

            for m in range(2):
                slot(m, m)
            with dve.Fori(1, NBLK // 2) as p:
                for par in range(2):
                    slot(p * 2 + par, par)
            slot(NBLK - 1, 0)
            block_act_t(NBLK - 1, 0)

            dve.wait_ge(s_sa, NCH + 1)
            for n in range(NCH):
                dve.wait_ge(s_yg[n], 16 * TOP * TC)
                for i, s_c in enumerate((s_c1, s_c2)):
                    for t in range(n * TC, n * TC + TC):
                        if i == 1:
                            dve.wait_ge(s_c1, t + 1)
                        dve.scalar_tensor_tensor(x_all[:, t], y_got[:, i, t], top_w[:, t, i:i + 1], x_all[:, t],
                                                 ALU.mult, ALU.add).then_inc(s_c, 1)

        @block.tensor
        def _(pe):
            pe.wait_ge(s_w, 16 * 11)

            def turn(b, half):
                n = b * 2 + half
                pe.wait_ge(s_xn, n + 1)
                for t in range(TC):
                    ins = pe.transpose(ps[0][:, t * P:t * P + P], xn[:, half, t * P:t * P + P], ident[:])
                ins.then_inc(s_xtp, 1)

            def project(b, half, last):
                n = b * 2 + half
                pe.wait_ge(s_xt, n + 1)
                pe.wait_ge(s_r1[0], n + 1)
                pe.matmul(ps[1][:], wq_p, xn_t[:, half], start=True, stop=True)
                pe.matmul(ps[2][:], wq_s, xn_t[:, half], start=True, stop=True).then_inc(s_qp, 1)
                pe.matmul(ps[3][0:L], wdn_sb, xn_t[:, half], start=True, stop=True).then_inc(s_lp, 1)
                if not last:
                    turn(b + (half + 1) // 2, (half + 1) % 2)
                pe.wait_ge(s_lt, n + 1)
                pe.wait_ge(s_r1[1], n + 1)
                pe.matmul(ps[4][:], wk_p[0:L], lat_t[0:L, half], start=True, stop=True)
                pe.matmul(ps[5][:], wk_s[0:L], lat_t[0:L, half], start=True, stop=True).then_inc(s_kp, 1)
                for t in range(TC):
                    ins = pe.matmul(ps[6][:, t * P:t * P + P], lat_t[0:L, half, t * P:t * P + P], wv_sb[0:L],
                                    start=True, stop=True)
                ins.then_inc(s_vp, 1)

            pe.wait_ge(s_wp, 18)
            turn(0, 0)
            with pe.Fori(0, B - 1) as b:
                for half in range(2):
                    project(b, half, False)
            for half in range(2):
                project(B - 1, half, half == 1)

            def max_score(i, k, n, ck, qt, heads):
                w = max_width(ck, qt)
                if not (isinstance(i, int) and i == 0 and n < 2):
                    pe.wait_ge(s_rd, i * NU + n - 1)
                for a, j in enumerate(heads):
                    ins = pe.matmul(ps[3 + n % 2][:, a * w:a * w + w], q_op[k][0:MAX_ROW, j, qt * P:qt * P + P],
                                    k_op[k][0:MAX_ROW, j, ck * W:ck * W + w], start=True, stop=True)
                ins.then_inc(s_s1, 1)

            def score(i, k, r, u):
                c, kt = ROUNDS[r]
                lo = low(c, kt)
                w, n = W - lo, CUM[r] + u
                if not (isinstance(i, int) and i == 0 and n < 3):
                    pe.wait_ge(s_ex, i * NU + n - 2)
                for a, j in enumerate(UNITS[r][u]):
                    ins = pe.matmul(ps[(NU * k + n) % 3][:, a * w:a * w + w],
                                    k_op[k][0:ROWS, j, kt * P:kt * P + P],
                                    q_op[k][0:ROWS, j, c * W + lo:c * W + W], start=True, stop=True)
                ins.then_inc(s_s2, 1)

            def add_values(i, k, r):
                c, kt = ROUNDS[r]
                lo = low(c, kt)
                pe.wait_ge(s_ex, i * NU + CUM[r + 1])
                if r == 0:
                    pe.wait_ge(s_vb, i + 1)
                for j in range(HG):
                    ins = pe.matmul(ps[5 + c][32 * j:32 * j + D + 1, lo:W],
                                    v_buf[:, k, kt, j * (D + 1):(j + 1) * (D + 1)], prob[:, r % 3, j, 0:W - lo],
                                    start=(kt == 0), stop=(kt == TC * (c + 1) - 1))
                ins.then_inc(s_pv, 1)

            def turn_max(i, c):
                if c == 0:
                    pe.wait_ge(s_rd, i * NU + MAX_BEFORE[3])
                    src = mx[:, 0].rearrange("p j t -> p (j t)")
                else:
                    pe.wait_ge(s_m1, i + 1)
                    src = mx1[:].rearrange("p j t -> p (j t)")
                pe.transpose(ps[7][0:HG * TC, 0:P], src, ident[:]).then_inc(s_mi, 1)

            def turn_out(c):
                for t in range(TC):
                    ins = pe.transpose(ps[7][:, t * P:t * P + P], o_sb[:, c, t * P:t * P + P], ident[:])
                ins.then_inc(s_mi, 1)

            pe.wait_ge(s_r1[0], NCH + 1)
            pe.wait_ge(s_r1[1], NCH + 1)
            pe.wait_ge(s_vr, NCH)
            pe.wait_ge(s_pc[0], 32)
            pe.wait_ge(s_ld[0], 16 * N_LD)
            for slot in range(NR):
                for n, ck, qt, heads in MAX_UNITS[slot]:
                    max_score(0, 0, n, ck, qt, heads)
            turn_max(0, 0)
            pe.wait_ge(s_mn, 1)
            turn_max(0, 1)
            pe.sem_inc(s_pv, 3)
            pe.wait_ge(s_z, 4)
            pe.wait_ge(s_mr[0], 16)
            for u in range(len(UNITS[0])):
                score(0, 0, 0, u)

            def group(i, k, last):
                nk = (k + 1) % 3
                lap = 16 * N_LD
                for r in range(NR):
                    if r == 0 and not last:
                        pe.wait_ge(s_pc[nk], 32)
                        pe.wait_ge(s_ld[nk], pe_lap(i, k) * lap)
                    si, sk, sr = (i, k, r + 1) if r + 1 < NR else (i + 1, nk, 0)
                    n2 = 0 if (r + 1 == NR and last) else len(UNITS[sr])
                    if n2 and sr in (0, TC):
                        pe.wait_ge(s_mr[0 if sr == 0 else 1], (si + 1) * 16)
                    mine = [] if last else MAX_UNITS[r]
                    for u in range(max(n2, len(mine))):
                        if u < n2:
                            score(si, sk, sr, u)
                        if u < len(mine):
                            max_score(i + 1, nk, *mine[u])
                    add_values(i, k, r)
                    if r == OT1_SLOT:
                        pe.wait_ge(s_ob[1], i + 1)
                        pe.wait_ge(s_mn, i * 2 + 2)
                        turn_out(1)
                    if r == OT0_SLOT:
                        pe.wait_ge(s_ob[0], i + 1)
                        pe.wait_ge(s_on, i * 2 + 2)
                        turn_out(0)
                    if r == MT0_SLOT and not last:
                        pe.wait_ge(s_on, i * 2 + 3)
                        turn_max(i + 1, 0)
                    if r == MT1_SLOT and not last:
                        pe.wait_ge(s_mn, i * 2 + 3)
                        turn_max(i + 1, 1)

            def pe_lap(i, k):
                if isinstance(i, int):
                    return (i + 1) // 3 + 1
                return lap_reg[0] + (1 if k < 2 else 2)

            lap_reg = [None]
            with pe.Fori(0, (NG - 1) // 3) as p:
                lap_reg[0] = p
                for k in range(3):
                    group(p * 3 + k, k, False)
            group(NG - 1, 0, True)
            pe.wait_ge(s_ob[1], NG + 1)
            pe.wait_ge(s_on, 2 * NG + 1)
            turn_out(1)

            pe.wait_ge(s_on, 2 * NG + 2)
            pe.transpose(ps[3][:, 0:NE], gw_row[:], ident[0:NE, 0:NE]).then_inc(s_gt, 1)
            pe.wait_ge(s_gc, 1)
            pe.sem_inc(s_atp, 2)

            def project_out(b, half):
                n = b * 2 + half
                pe.wait_ge(s_at, n + 1)
                for t in range(TC):
                    ins = pe.transpose(ps[0][:, t * P:t * P + P], a_tok[:, half, t * P:t * P + P], ident[:])
                ins.then_inc(s_atp, 1)
                pe.wait_ge(s_att, n + 1)
                pe.wait_ge(s_x1, n + 1)
                for t in range(TC):
                    ins = pe.matmul(ps[1][:, t * P:t * P + P], a_t[:, half, t * P:t * P + P], wo_sb[:],
                                    start=True, stop=True)
                ins.then_inc(s_y, 1)

            with pe.Fori(0, B) as b:
                for half in range(2):
                    project_out(b, half)

            def route(b, half):
                n = b * 2 + half
                pe.wait_ge(s_xn2, n + 1)
                for t in range(TC):
                    ins = pe.transpose(ps[2][:, t * P:t * P + P], xn2[:, half, t * P:t * P + P], ident[:])
                ins.then_inc(s_xp2, 1)
                pe.wait_ge(s_xk2, n + 1)
                pe.wait_ge(s_lc, n + 1)
                for t in range(TC):
                    ins = pe.matmul(ps[3][:, t * NE:t * NE + NE], xn2_c[:, half, t * P:t * P + P], gw_t[:],
                                    start=True, stop=True)
                ins.then_inc(s_lg, 1)

            with pe.Fori(0, B) as b:
                for half in range(2):
                    route(b, half)

            pe.wait_ge(s_z, 4)
            pe.wait_ge(s_pk, 1)
            rows = picked[:].rearrange("p t e -> p (t e)")
            pe.matmul(ps[4][:, 0:NT * NE], before_sb[:], rows, start=True, stop=True)
            pe.matmul(ps[5][:, 0:NT * NE], ones_sb[:], rows, start=True, stop=True).then_inc(s_cn, 1)

            pe.wait_ge(s_ew, 16 * (2 + NE + 3))
            pe.wait_ge(s_lc, NCH + 1)
            pe.sem_inc(s_dn, 2)
            with pe.Fori(0, NCH) as n:
                def down(s):
                    pe.wait_ge(s_ac, n * NSH + s + 3)
                    if s == 0:
                        pe.wait_ge(s_sa, n + 1)
                    for t in range(TC):
                        ins = pe.matmul(ps[6][:, t * P:t * P + P], act_t[:, s % 2, t * P:t * P + P], sd_sb[:, s],
                                        start=(s == 0 and t == 0), stop=(s == NSH - 1 and t == TC - 1),
                                        skip_group_check=True)
                    ins.then_inc(s_dn, 1)

                for s in range(NSH):
                    pe.wait_ge(s_ac, n * NSH + s + 1)
                    for w, bank in ((sg_sb, 0), (su_sb, 2)):
                        ins = pe.matmul(ps[bank + s % 2][:], w[:, s * P:s * P + P], xn2_t[:, n], start=True, stop=True)
                    ins.then_inc(s_h, 1)
                for s in range(NSH):
                    down(s)

            def expert(m):
                return pe.value_load(b_exp[0:1, bass.ds(m, 1)], min_val=0, max_val=NE - 1)

            def block_turn(m, par, lap):
                pe.wait_ge(s_bl[par], lap * 16 + 16)
                if not (isinstance(m, int) and m < 1):
                    pe.wait_ge(s_bt, m)
                pe.transpose(ps[0][:, 0:P], xb[:, par], ident[:]).then_inc(s_bx, 1)

            def block_hidden(m, par):
                pe.wait_ge(s_bt, m + 1)
                if not (isinstance(m, int) and m < 2):
                    pe.wait_ge(s_ba, m - 1)
                e = expert(m)
                pe.matmul(ps[1 + par][:], xb_t[:, par], wg_sb[:, e], start=True, stop=True).then_inc(s_bg, 1)
                pe.matmul(ps[3 + par][:], xb_t[:, par], wu_sb[:, e], start=True, stop=True).then_inc(s_bu, 1)

            def block_act_turn(m, par):
                pe.wait_ge(s_ba, m + 1)
                for c in range(F // P):
                    ins = pe.transpose(ps[5 + par][:, c * P:c * P + P], b_act[:, par, c * P:c * P + P], ident[:])
                ins.then_inc(s_bp, 1)

            def block_down(m, par):
                pe.wait_ge(s_bc, m + 1)
                pe.wait_ge(s_by, m + 1)
                e = expert(m)
                for c in range(F // P):
                    ins = pe.matmul(ps[7][:, 0:E], b_act_t[:, par, c * P:c * P + P], wd_sb[:, e, c],
                                    start=(c == 0), stop=(c == F // P - 1))
                ins.then_inc(s_bd, 1)

            def slot(m, par, lap):
                block_hidden(m, par)
                if not (isinstance(m, int) and m < 2):
                    block_down(m - 2, par)
                if not (isinstance(m, int) and m < 1):
                    block_act_turn(m - 1, 1 - par)
                if not (isinstance(m, int) and m + 1 >= NBLK):
                    block_turn(m + 1, 1 - par, lap + par)

            pe.wait_ge(s_sa, NCH + 1)
            pe.wait_ge(s_be, 1)
            block_turn(0, 0, 0)
            for m in range(2):
                slot(m, m, 0)
            with pe.Fori(1, NBLK // 2) as p:
                for par in range(2):
                    slot(p * 2 + par, par, p)
            slot(NBLK - 1, 0, NBLK // 2)
            block_down(NBLK - 2, 1)
            block_act_turn(NBLK - 1, 0)
            block_down(NBLK - 1, 0)


_INS = ['L0_attn_x', 'L0_attn_wq', 'L0_attn_w_down', 'L0_attn_wk_up', 'L0_attn_wv_up', 'L0_attn_wo',
        'L0_ffn_gate_w', 'L0_ffn_gate_k', 'L0_ffn_up_k', 'L0_ffn_down_k', 'L0_ffn_sh_gate', 'L0_ffn_sh_up',
        'L0_ffn_sh_down']


def shape_tables():
    inv = 1.0 / 10000.0 ** (np.arange(0, D, 2, dtype=np.float32) / D)
    ang = np.outer(np.arange(T, dtype=np.float32), inv)
    cos, sin = np.cos(ang).astype(np.float32), np.sin(ang).astype(np.float32)
    d = (np.arange(P) // HG) % D
    cos_t = cos[:, d // 2].T
    sin_t = sin[:, d // 2].T * np.where(d % 2 == 0, -1.0, 1.0).astype(np.float32)[:, None]
    page = np.arange(T) // PAGE
    rows = np.arange(NPAGE)[:, None]
    page_k = np.concatenate([page[None, :] == rows, np.ones((3, T))])
    page_q = np.where(page[None, :] < rows, NEG, 0.0)
    return {
        "cos_t": np.ascontiguousarray(cos_t, np.float32),
        "sin_t": np.ascontiguousarray(sin_t, np.float32),
        "page_k": (page_k.astype(np.float32).view(np.uint32) >> 16).astype(np.uint16),
        "page_q": (page_q.astype(np.float32).view(np.uint32) >> 16).astype(np.uint16),
        "eye": np.eye(P, dtype=np.float32),
        "before": np.triu(np.ones((P, P), np.float32), 1),
        "count_t": np.tile(np.concatenate([np.arange(NBLK), P * np.arange(MAXB)]).astype(np.float32), (P, 1)),
    }


def kernel(**inputs):
    import concourse.bacc as _bacc
    from concourse.bass_utils import run_bass_kernel_spmd as _run

    nc = _bacc.Bacc("TRN2", target_bir_lowering=False, num_devices=1)
    arrays, args = {}, []
    given = [(n, np.ascontiguousarray(inputs[n])) for n in _INS] + list(shape_tables().items())
    for name, a in given:
        arrays[f"in_{name}_dram"] = a
        args.append(nc.dram_tensor(f"in_{name}_dram", a.shape, mybir.dt.from_np(a.dtype), kind="ExternalInput").ap())
    out = nc.dram_tensor("out_0_dram", (B, T, E), F32, kind="ExternalOutput").ap()
    build(nc, *args, out)
    r = _run(nc, [arrays], core_ids=[0])
    return r.results[0]["out_0_dram"]
```

```python
from contextlib import ExitStack

import numpy as np

import concourse.bass as bass
from concourse import mybir

F32 = mybir.dt.float32
BF16 = mybir.dt.bfloat16
U32 = mybir.dt.uint32
I32 = mybir.dt.int32
ALU = mybir.AluOpType
ACT = mybir.ActivationFunctionType
AX = mybir.AxisListType

P = 128
B, T, E = 4, 1024, 128
H, D = 16, 8
HG = 4
GB = H // HG
NG = B * GB
L = 64
PAGE = 32
NPAGE = T // PAGE
W = 512
TC = W // P
NCH = B * T // W
NT = B * T // P
TB = T // P
NE, F, FS = 8, 512, 256
TOP = 2
NBLK = TOP * B * T // P + NE - 1
PLACES = NBLK * P
MAXB = B * T // P
EPS = 1e-5
SCALE = 1.0 / float(np.sqrt(D))
NEG = -1.0e30

Q_SLOTS = ((0, 3), (1, 3), (2, 2))
SLOT_ROWS = 8 * D
MASK_ROW = SLOT_ROWS
MAX_ROW = MASK_ROW + NPAGE
ROWS = MAX_ROW + 3

ROUNDS = [(c, kt) for c in range(T // W) for kt in range(TC * (c + 1))]
NR = len(ROUNDS)


def low(c, t):
    return max(0, P * t - W * c)


def packed(w):
    return 1 if w > W // 2 else W // w


def units_of(w):
    n = packed(w)
    return [list(range(h, h + n)) for h in range(0, HG, n)]


UNITS = [units_of(W - low(c, kt)) for c, kt in ROUNDS]
CUM = [sum(len(u) for u in UNITS[:r]) for r in range(NR + 1)]
NU = CUM[NR]

MAX_SLOTS = [[(0, 3)], [(0, 2)], [(0, 1), (0, 0)], [(0, 4)], [(0, 5)], [(0, 6)], [(0, 7)],
             [(1, 7)], [(1, 6)], [(1, 5), (1, 4)], [], []]


def max_width(ck, qt):
    return min(W, P * (qt + 1) - W * ck)


def max_units():
    n, out = 0, []
    for slot in MAX_SLOTS:
        here = []
        for ck, qt in slot:
            for heads in units_of(max_width(ck, qt)):
                here.append((n, ck, qt, heads))
                n += 1
        out.append(here)
    assert n == NU and n % 2 == 0
    return out


MAX_UNITS = max_units()
MAX_BEFORE = [sum(len(s) for s in MAX_UNITS[:i]) for i in range(NR + 1)]
OT1_SLOT, OT0_SLOT, MT0_SLOT, MT1_SLOT = 1, 5, 6, 11


def build(nc, x, wq, w_down, wk_up, wv_up, wo, gate_w, gate_k, up_k, down_k, sh_gate, sh_up, sh_down,
          cos_t, sin_t, page_k, page_q, eye, before, count_t, out):
    q_scr = nc.dram_tensor("q_scr", (NG, 3, D * HG, T), BF16).ap()
    k_scr = nc.dram_tensor("k_scr", (NG, 3, D * HG, T), BF16).ap()
    x_scr = nc.dram_tensor("x_scr", (PLACES, E), F32).ap()
    y_scr = nc.dram_tensor("y_scr", (PLACES, E), F32).ap()
    m_scr = nc.dram_tensor("m_scr", (NG, 2, 3, HG * W), BF16).ap()

    with ExitStack() as ctx:
        def sb(name, shape, dt=F32):
            return ctx.enter_context(nc.sbuf_tensor(name, shape, dt))

        def sem(name):
            return ctx.enter_context(nc.semaphore(name))

        ident = sb("ident", [P, P])
        x_all = sb("x_all", [P, NT, E])
        v_all = sb("v_all", [P, NG, TB, HG * (D + 1)])
        attn = sb("attn", [P, NG + 1, TB, HG * D])
        wo_sb = sb("wo_sb", [P, E])
        gw_row = sb("gw_row", [NE, E])
        gw_t = sb("gw_t", [P, NE])
        before_sb = sb("before_sb", [P, P])
        ones_sb = sb("ones_sb", [P, P])
        zero_sb = sb("zero_sb", [P, E])
        count_sb = sb("count_sb", [P, NBLK + MAXB])

        arena = sb("arena", [P, 3 * HG * T + 3 * HG * W])
        w_arena = sb("w_arena", [P, 3 * NE * F + 3 * FS])
        at = [0]

        def view(words, shape, dt=F32, start=None, of=arena):
            if start is not None:
                at[0] = start
            v = of[:, at[0]:at[0] + words]
            at[0] += words
            assert at[0] <= of.shape[1]
            if dt is not F32:
                v = v.bitcast(dt)
            if len(shape) == 2:
                v = v.rearrange("p (a b) -> p a b", a=shape[0])
            elif len(shape) == 3:
                v = v.rearrange("p (a b c) -> p a b c", a=shape[0], b=shape[1])
            return v

        cos_sb = view(T, (T,), start=0, of=w_arena)
        sin_sb = view(T, (T,), of=w_arena)
        xn = view(2 * W, (2, W), of=w_arena)
        xn_t = view(2 * W, (2, W), of=w_arena)
        rope_a = view(2 * W, (2, W), of=w_arena)
        rope_b = view(2 * W, (2, W), of=w_arena)
        roped = view(2 * W, (2, W), of=w_arena)
        rest = view(2 * W, (2, W), of=w_arena)
        parts = [view(2 * 3 * W // 2, (2, 3, W), BF16, of=w_arena) for _ in range(2)]
        wq_sb = view(E, (E,), of=w_arena)
        wq_p = view(E, (E,), of=w_arena)
        wq_s = view(E, (E,), of=w_arena)
        wk_up_sb = view(E, (E,), of=w_arena)
        wk_sb = view(E, (E,), of=w_arena)
        wk_p = view(E, (E,), of=w_arena)
        wk_s = view(E, (E,), of=w_arena)
        wv_up_sb = view(E, (E,), of=w_arena)
        wv_sb = view(E, (E,), of=w_arena)
        wdn_sb = view(L, (L,), of=w_arena)
        wdn_t = view(E, (E,), of=w_arena)
        wg_sb = view(NE * F, (NE, F), start=0, of=w_arena)
        wu_sb = view(NE * F, (NE, F), of=w_arena)
        wd_sb = view(NE * F, (NE, F // P, E), of=w_arena)
        sg_sb = view(FS, (FS,), of=w_arena)
        su_sb = view(FS, (FS,), of=w_arena)
        sd_sb = view(FS, (FS // P, E), of=w_arena)
        QK_WORDS = HG * T // 2
        q_op = [view(QK_WORDS, (HG, T), BF16, start=i * QK_WORDS) for i in range(3)]
        k_op = [view(QK_WORDS, (HG, T), BF16) for i in range(3)]
        prob = view(3 * HG * W, (3, HG, W))
        a_tok = view(2 * W, (2, W), start=0)
        a_t = view(2 * W, (2, W))
        xn2 = view(2 * W, (2, W))
        xn2_c = view(2 * W, (2, W))
        shared_at = at[0]
        xn2_all = view(NT * E, (NT, E))
        xn2_t = view(NCH * W, (NCH, W))
        silu = view(2 * W, (2, W))
        act_t = view(2 * W, (2, W))
        xb = view(2 * E, (2, E))
        xb_t = view(2 * P, (2, P))
        b_silu = view(2 * F, (2, F))
        b_act = view(2 * F, (2, F))
        b_act_t = view(2 * F, (2, F))
        yb = view(2 * E, (2, E))
        y_got = view(TOP * NT * E, (TOP, NT, E), start=shared_at)

        v_buf = sb("v_buf", [P, 3, TB, HG * (D + 1)])
        o_sb = sb("o_sb", [P, 2, W])
        o_rec = sb("o_rec", [P, TC * HG])
        mx = sb("mx", [P, 3, HG, TC])
        mx1 = sb("mx1", [P, HG, TC])
        m_neg = sb("m_neg", [HG * TC, 2, P])
        m_rest = sb("m_rest", [HG * TC, 2, P])
        m_part = sb("m_part", [HG * TC, 2, 3, P], BF16)

        st = sb("st", [P, NT, 6])
        mean = sb("mean", [P, NT])
        var = sb("var", [P, NT])
        dif = sb("dif", [P, NT])
        rstd = sb("rstd", [P, NT])
        logit = sb("logit", [P, TB, NE])
        top_v = sb("top_v", [P, TB, NE])
        top_i = sb("top_i", [P, TB, NE], U32)
        top_va = sb("top_va", [P, NT, NE])
        top_ia = sb("top_ia", [P, NT, 2])
        e_sum = sb("e_sum", [P, NT])
        top_w = sb("top_w", [P, NT, 2])
        pick = [sb(f"pick{i}", [P, NT, NE]) for i in range(TOP)]
        picked = sb("picked", [P, NT, NE])
        total = sb("total", [P, NT, NE])
        upto = [sb(f"upto{i}", [P, NT, NE]) for i in range(2)]
        over_k = sb("over_k", [P, NE, MAXB])
        blocks = sb("blocks", [P, NE])
        b_end = [sb(f"b_end{i}", [P, NE]) for i in range(2)]
        b_base = sb("b_base", [P, NE])
        place = sb("place", [P, NT, NE])
        place_f = [sb(f"place_f{i}", [P, NT]) for i in range(TOP)]
        place_u = [sb(f"place_u{i}", [P, NT], U32) for i in range(TOP)]
        b_past = sb("b_past", [1, NBLK, NE])
        b_exp_f = sb("b_exp_f", [1, NBLK])
        b_exp = sb("b_exp", [1, NBLK], I32)

        ps = [ctx.enter_context(nc.psum_tensor(f"ps{i}", [P, W], F32)) for i in range(8)]

        s_x = sem("x_loaded")
        s_w = sem("weights_loaded")
        s_ew = sem("expert_weights_loaded")
        s_vone = sem("v_ones_set")
        s_pc = [sem(f"page_rows_loaded{i}") for i in range(3)]
        s_st = sem("stats_done")
        s_d1 = sem("dve_step")
        s_a1 = sem("act_step")
        s_wp = sem("weights_permuted")
        s_xn = sem("xn_ready")
        s_xtp = sem("xn_turned")
        s_xt = sem("xn_t_ready")
        s_qp = sem("q_projected")
        s_wdp = sem("w_down_products")
        s_wdc = sem("w_down_products_copied")
        s_kp = sem("k_projected")
        s_vp = sem("v_projected")
        s_vr = sem("v_ready")
        s_rm = [sem("rope_q_products"), sem("rope_k_products")]
        s_rs = [sem("q_roped"), sem("k_roped")]
        s_p0 = [sem("q_part0"), sem("k_part0")]
        s_r1 = [sem("q_rest"), sem("k_rest")]
        s_p1 = [sem("q_part1"), sem("k_part1")]
        s_p2 = [sem("q_part2"), sem("k_part2")]
        s_sc = [[sem(f"{z}_parts{h}_stored") for h in range(2)] for z in "qk"]
        s_ld = [sem(f"qk_loaded{i}") for i in range(3)]
        s_s1 = sem("max_scores")
        s_rd = sem("max_reduced")
        s_m1 = sem("max_joined")
        s_trn = sem("sums_or_maxima_turned")
        s_pass = [sem("dve_passed"), sem("pool_passed")]
        s_mn = sem("minus_max")
        s_ms = sem("minus_max_step")
        s_mw = [sem("max_rows_out0"), sem("max_rows_out1")]
        s_mr = [sem("max_rows_in0"), sem("max_rows_in1")]
        s_s2 = sem("scores")
        s_ex = sem("probs")
        s_pv = sem("values_added")
        s_vb = sem("v_buf_ready")
        s_ob = [sem("o_copied0"), sem("o_copied1")]
        s_or = sem("o_reciprocal")
        s_on = sem("attn_ready")
        s_z = sem("zeroed")
        s_at = sem("attn_staged")
        s_atp = sem("attn_turned")
        s_att = sem("attn_t_ready")
        s_y = sem("attn_projected")
        s_x1 = sem("residual_added")
        s_st2 = sem("stats2")
        s_xn2 = sem("xn2_ready")
        s_xp2 = sem("xn2_turned")
        s_xc2 = sem("xn2_t_ready")
        s_xk2 = sem("xn2_t_kept")
        s_xk = sem("xn2_kept")
        s_lg = sem("logits")
        s_lc = sem("logits_copied")
        s_mxv = sem("top_values")
        s_mxi = sem("top_indices")
        s_tk = sem("top_kept")
        s_gt = sem("gate_w_turned")
        s_gc = sem("gate_w_t_ready")
        s_pk = sem("picked_ready")
        s_cn = sem("picked_counted")
        s_pl = sem("places_ready")
        s_be = sem("block_experts_ready")
        s_h = sem("shared_hidden")
        s_si = sem("shared_silu")
        s_ac = sem("shared_act")
        s_dn = sem("shared_down")
        s_sa = sem("shared_added")
        s_xz = sem("x_scr_cleared")
        s_xs = sem("tokens_scattered")
        s_bl = [sem(f"block_loaded{i}") for i in range(2)]
        s_bx = sem("block_turned")
        s_bt = sem("block_t_ready")
        s_bg = sem("block_gate")
        s_bu = sem("block_up")
        s_bs = sem("block_silu")
        s_ba = sem("block_act")
        s_bp = sem("block_act_turned")
        s_bc = sem("block_act_t_ready")
        s_bd = sem("block_down")
        s_by = sem("block_out_copied")
        s_bo = [sem(f"block_stored{i}") for i in range(2)]
        s_yg = [sem(f"outputs_gathered{n}") for n in range(NCH)]
        s_c1 = sem("first_expert_added")
        s_c2 = sem("second_expert_added")
        s_out = sem("out_stored")

        block = ctx.enter_context(nc.Block())

        x_v = x.rearrange("b (n p) e -> p (b n) e", p=P)
        out_v = out.rearrange("b (n p) e -> p (b n) e", p=P)
        NSH = FS // P
        N_LD = 5

        @block.sync
        def _(sp):
            sp.dma_start(x_all[:, 0:NT // 2], x_v[:, 0:NT // 2]).then_inc(s_x, 16)
            sp.dma_start(x_all[:, NT // 2:NT], x_v[:, NT // 2:NT]).then_inc(s_x, 16)
            small = [(ident[:], eye), (wdn_sb, w_down), (wk_up_sb[0:L], wk_up), (wv_up_sb[0:L], wv_up), (wq_sb, wq),
                     (cos_sb, cos_t), (sin_sb, sin_t), (wo_sb[:], wo), (gw_row[:], gate_w), (before_sb[:], before),
                     (count_sb[:], count_t)]
            for dst, src in small:
                sp.dma_start(dst, src).then_inc(s_w, 16)
            sp.wait_ge(s_z, 4)
            sp.dma_start(x_scr.rearrange("(m p) e -> p m e", p=P),
                         zero_sb[:].unsqueeze(1).to_broadcast([P, NBLK, E])).then_inc(s_xz, 16)

            def store_parts(b, half):
                n = b * 2 + half
                for z, scr in enumerate((q_scr, k_scr)):
                    sp.wait_ge(s_p2[z], n + 1)
                    for g in range(GB):
                        sp.dma_start(scr[b * GB + g, :, :, half * W:half * W + W].rearrange("a r t -> r a t"),
                                     parts[half][32 * g:32 * g + 32, z]).then_inc(s_sc[z][half], 16)

            for z in range(2):
                for half in range(2):
                    sp.sem_inc(s_sc[z][half], 1)
            for i in range(3):
                for dst, src in ((q_op[i], page_q), (k_op[i], page_k)):
                    n = src.shape[0]
                    sp.dma_start(dst[MASK_ROW:MASK_ROW + n],
                                 src.bitcast(BF16).unsqueeze(1).to_broadcast([n, HG, T])).then_inc(s_pc[i], 16)

            def load(i, buf):
                row = 0
                for part, n in Q_SLOTS:
                    src = q_scr[i, part].rearrange("(d j) t -> d (j t)", d=D).unsqueeze(0)
                    sp.dma_start(q_op[buf][row:row + n * D].rearrange("r j t -> r (j t)"),
                                 src.to_broadcast([n, D, HG * T])).then_inc(s_ld[buf], 16)
                    row += n * D
                src = k_scr[i].rearrange("a (d j) t -> (a d) (j t)", d=D)
                sp.dma_start(k_op[buf][0:6 * D].rearrange("r j t -> r (j t)"),
                             src.unsqueeze(0).to_broadcast([2, 3 * D, HG * T])).then_inc(s_ld[buf], 16)
                sp.dma_start(k_op[buf][6 * D:8 * D].rearrange("r j t -> r (j t)"),
                             src[0:2 * D]).then_inc(s_ld[buf], 16)

            def max_rows(i, buf, c):
                sp.wait_ge(s_ms, (i * 2 + c + 1) * 4)
                sp.dma_start(m_scr[i, c].rearrange("a (r n) -> r a n", n=P), m_part[:, c]).then_inc(s_mw[c], 16)
                sp.wait_ge(s_mw[c], (i + 1) * 16)
                sp.dma_start(q_op[buf][MAX_ROW:MAX_ROW + 3, :, c * W:c * W + W],
                             m_scr[i, c].rearrange("a (j t) -> a j t", j=HG)).then_inc(s_mr[c], 16)

            for half in range(2):
                store_parts(0, half)
            for z in range(2):
                for half in range(2):
                    sp.wait_ge(s_sc[z][half], 16 * GB + 1)
            for i in range(3):
                load(i, i)
            with sp.Fori(1, B) as b:
                for half in range(2):
                    store_parts(b, half)
            for z in range(2):
                for half in range(2):
                    sp.wait_ge(s_sc[z][half], 16 * GB * B + 1)
            sp.wait_ge(s_vr, NCH + 1)
            sp.dma_start(wg_sb, gate_k.rearrange("e d f -> d e f")).then_inc(s_ew, 16)
            sp.dma_start(wu_sb, up_k.rearrange("e d f -> d e f")).then_inc(s_ew, 16)
            for e in range(NE):
                sp.dma_start(wd_sb[:, e], down_k[e].rearrange("(c p) d -> p c d", p=P)).then_inc(s_ew, 16)
            sp.dma_start(sg_sb, sh_gate).then_inc(s_ew, 16)
            sp.dma_start(su_sb, sh_up).then_inc(s_ew, 16)
            sp.dma_start(sd_sb, sh_down.rearrange("(c p) d -> p c d", p=P)).then_inc(s_ew, 16)

            for c in range(2):
                max_rows(0, 0, c)

            def group(i, k, more):
                max_rows(i + 1, (k + 1) % 3, 0)
                max_rows(i + 1, (k + 1) % 3, 1)
                if more:
                    sp.wait_ge(s_s2, (i + 1) * NU)
                    load(i + 3, k)

            with sp.Fori(0, 4) as p:
                for k in range(3):
                    group(p * 3 + k, k, True)
            for i in range(12, NG - 1):
                group(i, i % 3, i + 3 < NG)

            def block_in(m, par):
                sp.dma_start(xb[:, par], x_scr[bass.ds(m * P, P), :]).then_inc(s_bl[par], 16)

            def block_out(m, par):
                sp.wait_ge(s_by, m + 2)
                sp.dma_start(y_scr[bass.ds(m * P, P), :], yb[:, par]).then_inc(s_bo[par], 16)

            sp.wait_ge(s_xs, 16 * TOP * NT)
            for par in range(2):
                sp.sem_inc(s_bo[par], 1)
                block_in(par, par)

            def slot(m, par):
                sp.wait_ge(s_bx, m + 1)
                block_in(m + 2, par)
                if not (isinstance(m, int) and m < 2):
                    block_out(m - 2, par)

            slot(0, 0)
            slot(1, 1)
            slot(2, 0)
            with sp.Fori(1, (NBLK - 3) // 2) as p:
                for par in (1, 0):
                    slot(p * 2 + (1 if par else 2), par)
            for m in range(NBLK - 4, NBLK):
                block_out(m, m % 2)

            for n in range(NCH):
                sp.wait_ge(s_c2, TC * (n + 1))
                sp.dma_start(out_v[:, n * TC:n * TC + TC], x_all[:, n * TC:n * TC + TC]).then_inc(s_out, 16)
            sp.wait_ge(s_out, 16 * NCH)

        @block.gpsimd
        def _(pool):
            def own_wait(s, value):
                pool.wait_ge(s, value)
                pool.sem_inc(s_pass[1], 1)

            pool.memset(v_all[:], 1.0).then_inc(s_vone, 1)
            pool.memset(ones_sb[:], 1.0).then_inc(s_z, 1)
            pool.memset(zero_sb[:], 0.0).then_inc(s_z, 1)

            def project(b, half):
                n = b * 2 + half
                for z in range(2):
                    pool.wait_ge(s_rm[z], n + 2)
                    pool.wait_ge(s_r1[z], n + 1)
                    pool.tensor_tensor(roped[:, z], rope_a[:, z], rope_b[:, z], ALU.add).then_inc(s_rs[z], 1)
                for z in range(2):
                    pool.wait_ge(s_p1[z], n + 1)
                    pool.tensor_tensor(parts[half][:, z, 2], rest[:, z], parts[half][:, z, 1],
                                       ALU.subtract).then_inc(s_p2[z], 1)

            with pool.Fori(0, B) as b:
                for half in range(2):
                    project(b, half)

            def values(i, buf):
                pool.tensor_copy(v_buf[:, buf], v_all[:, i]).then_inc(s_vb, 1)

            def split(i, c):
                k = (i * 2 + c) * 4
                own_wait(s_mn, i * 2 + c + 1)
                pool.tensor_copy(m_part[:, c, 0], m_neg[:, c]).then_inc(s_ms, 1)
                pool.wait_ge(s_ms, k + 1)
                pool.tensor_tensor(m_rest[:, c], m_neg[:, c], m_part[:, c, 0], ALU.subtract).then_inc(s_ms, 1)
                own_wait(s_ms, k + 2)
                pool.tensor_copy(m_part[:, c, 1], m_rest[:, c]).then_inc(s_ms, 1)
                pool.wait_ge(s_ms, k + 3)
                pool.tensor_tensor(m_part[:, c, 2], m_rest[:, c], m_part[:, c, 1],
                                   ALU.subtract).then_inc(s_ms, 1)

            pool.wait_ge(s_vr, NCH + 1)
            values(0, 0)
            for c in range(2):
                split(0, c)

            def group(i, k):
                own_wait(s_pv, i * NR + 3)
                values(i + 1, (k + 1) % 3)
                for c in range(2):
                    own_wait(s_mw[c], (i + 1) * 16)
                    split(i + 1, c)

            with pool.Fori(0, (NG - 1) // 3) as p:
                for k in range(3):
                    group(p * 3 + k, k)

            pool.wait_ge(s_on, 2 * NG + 1)

            def stage(b, half):
                n = b * 2 + half
                own_wait(s_atp, n + 1)
                pool.tensor_copy(a_tok[:, half].rearrange("p (t g e) -> p t g e", t=TC, g=GB),
                                 attn[:, bass.ds(b * GB + 1, GB), half * TC:half * TC + TC]
                                 .rearrange("p g t e -> p t g e")).then_inc(s_at, 1)

            with pool.Fori(0, B) as b:
                for half in range(2):
                    stage(b, half)

            with pool.Fori(0, B) as b:
                for half in range(2):
                    own_wait(s_xn2, b * 2 + half + 1)
                    pool.tensor_copy(xn2_all[:, bass.ds((b * 2 + half) * TC, TC)],
                                     xn2[:, half].rearrange("p (t e) -> p t e", e=E)).then_inc(s_xk, 1)

            pool.wait_ge(s_xk, NCH)
            pool.wait_ge(s_pl, 2)
            pool.wait_ge(s_xz, 16)
            for t in range(NT):
                for i in range(TOP):
                    pool.indirect_dma_start(x_scr, bass.IndirectOffsetOnAxis(ap=place_u[i][:, t:t + 1], axis=0),
                                            xn2_all[:, t], None, bounds_check=PLACES - 1).then_inc(s_xs, 16)

            for par in range(2):
                pool.wait_ge(s_bo[par], 16 * ((NBLK + 1 - par) // 2) + 1)
            for t in range(NT):
                for i in range(TOP):
                    pool.indirect_dma_start(y_got[:, i, t], None, y_scr,
                                            bass.IndirectOffsetOnAxis(ap=place_u[i][:, t:t + 1], axis=0),
                                            bounds_check=PLACES - 1).then_inc(s_yg[t // TC], 16)

        @block.scalar
        def _(act):
            def turn(b, half):
                n = b * 2 + half
                act.wait_ge(s_xtp, n + 1)
                act.activation(xn_t[:, half], ps[0][:], ACT.Copy).then_inc(s_xt, 1)

            def project(b, half, last):
                n = b * 2 + half
                if not last:
                    turn(b + (half + 1) // 2, (half + 1) % 2)
                act.wait_ge(s_vp, n + 1)
                for g in range(GB):
                    ins = act.activation(
                        v_all[:, b * GB + g, half * TC:half * TC + TC].rearrange("p t (j e) -> p t j e", j=HG)[:, :, :, 0:D],
                        ps[6][:].rearrange("p (t g j d) -> p t g j d", t=TC, g=GB, j=HG)[:, :, g], ACT.Copy)
                ins.then_inc(s_vr, 1)
                for z in range(2):
                    act.wait_ge(s_rs[z], n + 1)
                    act.wait_ge(s_sc[z][half], b * (16 * GB) + 1)
                    act.activation(parts[half][:, z, 0], roped[:, z], ACT.Copy).then_inc(s_p0[z], 1)
                for z in range(2):
                    act.wait_ge(s_r1[z], n + 2)
                    act.activation(parts[half][:, z, 1], rest[:, z], ACT.Copy).then_inc(s_p1[z], 1)

            act.sem_inc(s_vr, 1)
            act.wait_ge(s_wdp, 1)
            act.activation(wdn_t[0:L], ps[3][0:L, 0:E], ACT.Copy).then_inc(s_wdc, 1)
            act.wait_ge(s_wdp, 2)
            act.activation(wk_sb, ps[4][:, 0:E], ACT.Copy).then_inc(s_wdc, 1)
            act.activation(wv_sb, ps[4][:, E:2 * E], ACT.Copy).then_inc(s_wdc, 1)
            act.wait_ge(s_d1, 6)
            act.activation(rstd[:], var[:], ACT.Sqrt).then_inc(s_a1, 1)
            act.wait_ge(s_vone, 1)
            turn(0, 0)
            with act.Fori(0, B - 1) as b:
                for half in range(2):
                    project(b, half, False)
            for half in range(2):
                project(B - 1, half, half == 1)

            def exps(i, k, r):
                c, kt = ROUNDS[r]
                w = W - low(c, kt)
                for u, heads in enumerate(UNITS[r]):
                    n = CUM[r] + u
                    act.wait_ge(s_s2, i * NU + n + 1)
                    if u == 0:
                        act.wait_ge(s_pv, i * NR + r + 1)
                    act.activation(prob[:, r % 3, heads[0]:heads[0] + len(heads), 0:w],
                                   ps[(NU * k + n) % 3][:, 0:len(heads) * w].rearrange("p (j t) -> p j t", t=w),
                                   ACT.Exp, scale=SCALE).then_inc(s_ex, 1)

            def outputs(i, c):
                act.wait_ge(s_pv, i * NR + (TC if c == 0 else NR) + 3)
                act.activation(o_sb[:, c], ps[5 + c][:], ACT.Copy).then_inc(s_ob[c], 1)

            act.wait_ge(s_z, 4)
            exps(0, 0, 0)

            def group(i, k, last):
                for r in range(NR):
                    if r + 1 < NR:
                        exps(i, k, r + 1)
                    elif not last:
                        exps(i + 1, (k + 1) % 3, 0)
                    if r == 0:
                        outputs(i - 1, 1)
                    if r == TC:
                        outputs(i, 0)

            with act.Fori(0, (NG - 1) // 3) as p:
                for k in range(3):
                    group(p * 3 + k, k, False)
            group(NG - 1, 0, True)
            outputs(NG - 1, 1)

            def project_out(b, half):
                n = b * 2 + half
                act.wait_ge(s_atp, n + 3)
                act.activation(a_t[:, half], ps[5 * half][:], ACT.Copy).then_inc(s_att, 1)

            with act.Fori(0, B) as b:
                for half in range(2):
                    project_out(b, half)
            act.wait_ge(s_d1, 14)
            act.activation(rstd[:], var[:], ACT.Sqrt).then_inc(s_a1, 1)

            def keep(b, half):
                n = b * 2 + half
                act.wait_ge(s_xp2, n + 1)
                act.activation(xn2_c[:, half], ps[2 + 4 * half][:], ACT.Copy).then_inc(s_xc2, 1)
                act.activation(xn2_t[:, n], ps[2 + 4 * half][:], ACT.Copy).then_inc(s_xk2, 1)

            with act.Fori(0, B) as b:
                for half in range(2):
                    keep(b, half)

            act.wait_ge(s_d1, 18)
            act.activation(top_va[:], top_va[:], ACT.Exp).then_inc(s_a1, 1)

            with act.Fori(0, NCH) as n:
                for s in range(NSH):
                    act.wait_ge(s_h, n * NSH + s + 1)
                    act.wait_ge(s_ac, n * NSH + s + 1)
                    act.activation(silu[:, s % 2], ps[s % 2][:], ACT.Silu).then_inc(s_si, 1)

            def block_t(m, par):
                act.wait_ge(s_bx, m + 1)
                act.activation(xb_t[:, par], ps[0][:, 0:P], ACT.Copy).then_inc(s_bt, 1)

            def block_silu(m, par):
                act.wait_ge(s_bg, m + 1)
                if not (isinstance(m, int) and m < 2):
                    act.wait_ge(s_ba, m - 1)
                act.activation(b_silu[:, par], ps[1 + par][:], ACT.Silu).then_inc(s_bs, 1)

            def block_y(m, par, lap):
                act.wait_ge(s_bd, m + 1)
                act.wait_ge(s_bo[par], lap * 16 + 1)
                act.activation(yb[:, par], ps[7][:, 0:E], ACT.Copy).then_inc(s_by, 1)

            def slot(m, par, lap):
                block_silu(m, par)
                if not (isinstance(m, int) and m + 1 >= NBLK):
                    block_t(m + 1, 1 - par)
                if not (isinstance(m, int) and m < 2):
                    block_y(m - 2, par, lap - 1)

            act.sem_inc(s_by, 1)
            block_t(0, 0)
            for m in range(2):
                slot(m, m, 0)
            with act.Fori(1, NBLK // 2) as p:
                for par in range(2):
                    slot(p * 2 + par, par, p)
            slot(NBLK - 1, 0, NBLK // 2)
            block_y(NBLK - 2, 1, (NBLK - 2) // 2)
            block_y(NBLK - 1, 0, (NBLK - 1) // 2)

        @block.vector
        def _(dve):
            step = [0]

            def chain(ins):
                step[0] += 1
                ins.then_inc(s_d1, 1)
                dve.wait_ge(s_d1, step[0])

            def own_wait(s, value):
                dve.wait_ge(s, value)
                dve.sem_inc(s_pass[0], 1)

            for c in range(2):
                dve.memset(ps[5 + c][:], 1.0).then_inc(s_z, 1)
            dve.sem_inc(s_r1[0], 1)
            dve.sem_inc(s_r1[1], 1)
            dve.sem_inc(s_rm[0], 1)
            dve.sem_inc(s_rm[1], 1)
            dve.sem_inc(s_on, 1)
            dve.sem_inc(s_ac, 2)
            dve.sem_inc(s_sa, 1)
            dve.sem_inc(s_x1, 2)
            dve.sem_inc(s_lc, 1)
            dve.wait_ge(s_x, 32)
            with dve.Fori(0, NCH) as n:
                for t in range(TC):
                    ins = dve.bn_stats(st[:, n * TC + t], x_all[:, n * TC + t])
                ins.then_inc(s_st, 1)

            def permute(full, perm, swap):
                dve.tensor_copy(perm.rearrange("e (g d j) -> e g d j", g=GB, d=D),
                                full.rearrange("e (g j d) -> e g d j", g=GB, d=D)).then_inc(s_wp, 1)
                a = swap.rearrange("e (g i s j) -> e s g i j", g=GB, i=D // 2, s=2)
                b_ = full.rearrange("e (g j i s) -> e s g i j", g=GB, i=D // 2, s=2)
                for s in range(2):
                    for g in range(GB):
                        dve.tensor_copy(a[:, s, g], b_[:, 1 - s, g]).then_inc(s_wp, 1)

            dve.wait_ge(s_w, 16 * 11)
            permute(wq_sb, wq_p, wq_s)
            dve.wait_ge(s_wdc, 2)
            permute(wk_sb, wk_p, wk_s)
            dve.wait_ge(s_st, NCH)

            def moments(turn):
                chain(dve.tensor_tensor(mean[:], st[:, :, 1], st[:, :, 4], ALU.add))
                chain(dve.tensor_tensor(dif[:], st[:, :, 1], st[:, :, 4], ALU.subtract))
                chain(dve.tensor_tensor(var[:], st[:, :, 2], st[:, :, 5], ALU.add))
                chain(dve.tensor_tensor(dif[:], dif[:], dif[:], ALU.mult))
                chain(dve.tensor_scalar(var[:], var[:], 1.0 / E, EPS, ALU.mult, ALU.add))
                chain(dve.scalar_tensor_tensor(var[:], dif[:], 0.25, var[:], ALU.mult, ALU.add))
                dve.wait_ge(s_a1, turn)
                chain(dve.reciprocal(rstd[:], rstd[:]))
                chain(dve.tensor_scalar(mean[:], mean[:], 0.5, None, ALU.mult))

            moments(1)

            def normalise(b, half):
                n = b * 2 + half
                for t in range(TC):
                    k = n * TC + t
                    ins = dve.tensor_scalar(xn[:, half, t * P:t * P + P], x_all[:, k],
                                            mean[:, bass.ds(k, 1)], rstd[:, bass.ds(k, 1)],
                                            ALU.subtract, ALU.mult)
                ins.then_inc(s_xn, 1)

            def project(b, half, last):
                n = b * 2 + half
                if not last:
                    normalise(b + (half + 1) // 2, (half + 1) % 2)
                for z, (s_pj, bank) in enumerate(((s_qp, 1), (s_kp, 4))):
                    dve.wait_ge(s_pj, n + 1)
                    dve.tensor_tensor(rope_a[:, z], ps[bank][:], cos_sb[:, half * W:half * W + W], ALU.mult)
                    dve.tensor_tensor(rope_b[:, z], ps[bank + 1][:], sin_sb[:, half * W:half * W + W],
                                      ALU.mult).then_inc(s_rm[z], 1)
                for z in range(2):
                    dve.wait_ge(s_p0[z], n + 1)
                    dve.tensor_tensor(rest[:, z], roped[:, z], parts[half][:, z, 0], ALU.subtract).then_inc(s_r1[z], 1)

            normalise(0, 0)
            with dve.Fori(0, B - 1) as b:
                for half in range(2):
                    project(b, half, False)
            for half in range(2):
                project(B - 1, half, half == 1)

            def reduce(i, slot):
                for n, ck, qt, heads in MAX_UNITS[slot]:
                    w = max_width(ck, qt)
                    dve.wait_ge(s_s1, i * NU + n + 1)
                    dve.tensor_reduce(mx[:, 0 if qt < TC else 1 + ck, heads[0]:heads[0] + len(heads), qt % TC],
                                      ps[3 + n % 2][:, 0:len(heads) * w].rearrange("p (j t) -> p j t", t=w),
                                      AX.X, ALU.max).then_inc(s_rd, 1)

            def join(i):
                dve.wait_ge(s_rd, (i + 1) * NU)
                dve.tensor_tensor(mx1[:], mx[:, 1], mx[:, 2], ALU.max).then_inc(s_m1, 1)

            def negate(i, c, event):
                dve.wait_ge(s_trn, event + 1)
                dve.tensor_scalar(m_neg[:, c], ps[7][0:HG * TC, 0:P], -1.0, None, ALU.mult).then_inc(s_mn, 1)

            def finish(i, c, place, event):
                dve.wait_ge(s_trn, event + 1)
                o = ps[7][:].rearrange("p (a e) -> p a e", e=32)
                dve.reciprocal(o_rec[:], o[:, :, D]).then_inc(s_or, 1)
                dve.wait_ge(s_or, i * 2 + (1 if c == 1 else 2))
                dve.tensor_tensor(attn[:, place, c * TC:c * TC + TC].rearrange("p t (j d) -> p (t j) d", j=HG),
                                  o[:, :, 0:D], o_rec[:].unsqueeze(2).to_broadcast([P, TC * HG, D]),
                                  ALU.mult).then_inc(s_on, 1)
            for slot in range(NR):
                reduce(0, slot)
            join(0)
            for c in range(2):
                negate(0, c, c)

            def group(i, k, last):
                ev = i * 4 + 2
                for r in range(NR):
                    if not last:
                        reduce(i + 1, r)
                        if r + 1 == MT1_SLOT:
                            join(i + 1)
                    if r == OT1_SLOT:
                        finish(i, 1, i, ev)
                    if r == OT0_SLOT:
                        finish(i, 0, i + 1, ev + 1)
                    if r == MT0_SLOT and not last:
                        dve.wait_ge(s_ms, (i * 2 + 1) * 4)
                        negate(i + 1, 0, ev + 2)
                    if r == MT1_SLOT and not last:
                        dve.wait_ge(s_ms, (i * 2 + 2) * 4)
                        negate(i + 1, 1, ev + 3)

            with dve.Fori(0, (NG - 1) // 3) as p:
                for k in range(3):
                    group(p * 3 + k, k, False)
            group(NG - 1, 0, True)
            finish(NG, 1, NG, 4 * (NG - 1) + 4)

            dve.wait_ge(s_gt, 1)
            dve.tensor_copy(gw_t[:], ps[3][:, 0:NE]).then_inc(s_gc, 1)

            def project_out(b, half):
                n = b * 2 + half
                k = n * TC
                dve.wait_ge(s_y, n + 1)
                dve.tensor_tensor(x_all[:, bass.ds(k, TC)], ps[1 + 3 * half][:].rearrange("p (t e) -> p t e", e=E),
                                  x_all[:, bass.ds(k, TC)], ALU.add).then_inc(s_x1, 1)
                own_wait(s_x1, n + 3)
                for t in range(TC):
                    ins = dve.bn_stats(st[:, k + t], x_all[:, k + t])
                ins.then_inc(s_st2, 1)

            with dve.Fori(0, B) as b:
                for half in range(2):
                    project_out(b, half)
            dve.wait_ge(s_st2, NCH)
            moments(2)

            def choose(b, half):
                n = b * 2 + half
                k = n * TC
                if not isinstance(b, int) or n > 1:
                    dve.wait_ge(s_xk, n - 1)
                    dve.wait_ge(s_xp2, n - 1)
                for t in range(TC):
                    ins = dve.tensor_scalar(xn2[:, half, t * P:t * P + P], x_all[:, k + t],
                                            mean[:, bass.ds(k + t, 1)], rstd[:, bass.ds(k + t, 1)],
                                            ALU.subtract, ALU.mult)
                ins.then_inc(s_xn2, 1)

            def top(b):
                k = b * TB
                dve.wait_ge(s_lg, b * 2 + 2)
                dve.tensor_copy(logit[:], ps[3][:, 0:TB * NE].rearrange("p (t e) -> p t e", e=NE)).then_inc(s_lc, 1)
                own_wait(s_lc, b + 2)
                for t in range(TB):
                    ins = dve.max(top_v[:, t], logit[:, t])
                ins.then_inc(s_mxv, 1)
                own_wait(s_mxv, b + 1)
                for t in range(TB):
                    ins = dve.max_index(top_i[:, t], top_v[:, t], logit[:, t])
                ins.then_inc(s_mxi, 1)
                dve.tensor_copy(top_va[:, bass.ds(k, TB)], top_v[:])
                dve.wait_ge(s_mxi, b + 1)
                dve.tensor_copy(top_ia[:, bass.ds(k, TB)], top_i[:, :, 0:2]).then_inc(s_tk, 1)

            choose(0, 0)
            choose(0, 1)
            with dve.Fori(0, B - 1) as b:
                for half in range(2):
                    choose(b + 1, half)
                top(b)
            top(B - 1)
            dve.wait_ge(s_tk, B)

            def over(a, n=NE):
                return a.to_broadcast([P, NT, n])

            chain(dve.tensor_copy(e_sum[:], top_va[:, :, 0]))
            chain(dve.tensor_tensor(top_va[:], top_va[:], over(e_sum[:].unsqueeze(2)), ALU.subtract))
            every = count_sb[:, 0:NE].unsqueeze(1).to_broadcast([P, NT, NE])
            for i in range(TOP):
                chain(dve.tensor_tensor(pick[i][:], every, over(top_ia[:, :, i:i + 1]), ALU.is_equal))
            dve.tensor_tensor(picked[:], pick[0][:], pick[1][:], ALU.add).then_inc(s_pk, 1)
            dve.wait_ge(s_a1, 3)
            chain(dve.tensor_reduce(e_sum[:], top_va[:], AX.X, ALU.add))
            chain(dve.reciprocal(e_sum[:], e_sum[:]))
            chain(dve.tensor_tensor(top_w[:], top_va[:, :, 0:2], over(e_sum[:].unsqueeze(2), 2), ALU.mult))

            dve.wait_ge(s_cn, 1)
            chain(dve.tensor_copy(total[:], ps[5][:, 0:NT * NE].rearrange("p (t e) -> p t e", e=NE)))
            a, z, k = total, 0, 1
            while k < NT:
                chain(dve.tensor_tensor(upto[z][:, k:NT], a[:, k:NT], a[:, 0:NT - k], ALU.add))
                chain(dve.tensor_copy(upto[z][:, 0:k], a[:, 0:k]))
                a, z, k = upto[z], 1 - z, 2 * k
            chain(dve.tensor_tensor(over_k[:], a[:, NT - 1].unsqueeze(2).to_broadcast([P, NE, MAXB]),
                                    count_sb[:, NBLK:NBLK + MAXB].unsqueeze(1).to_broadcast([P, NE, MAXB]),
                                    ALU.is_gt))
            chain(dve.tensor_reduce(blocks[:], over_k[:], AX.X, ALU.add))
            c, k, y = blocks, 1, 0
            while k < NE:
                chain(dve.tensor_tensor(b_end[y][:, k:NE], c[:, k:NE], c[:, 0:NE - k], ALU.add))
                chain(dve.tensor_copy(b_end[y][:, 0:k], c[:, 0:k]))
                c, k, y = b_end[y], 2 * k, 1 - y
            chain(dve.tensor_tensor(b_base[:], c[:], blocks[:], ALU.subtract))
            chain(dve.tensor_scalar(b_base[:], b_base[:], float(P), None, ALU.mult))
            chain(dve.tensor_tensor(place[:], a[:], total[:], ALU.subtract))
            chain(dve.tensor_tensor(place[:], place[:], b_base[:].unsqueeze(1).to_broadcast([P, NT, NE]), ALU.add))
            chain(dve.tensor_tensor(place[:], ps[4][:, 0:NT * NE].rearrange("p (t e) -> p t e", e=NE), place[:],
                                    ALU.add))
            for i in range(TOP):
                chain(dve.tensor_tensor(pick[i][:], pick[i][:], place[:], ALU.mult))
                chain(dve.tensor_reduce(place_f[i][:], pick[i][:], AX.X, ALU.add))
                dve.tensor_copy(place_u[i][:], place_f[i][:]).then_inc(s_pl, 1)
            chain(dve.tensor_tensor(b_past[:], c[0:1].unsqueeze(1).to_broadcast([1, NBLK, NE]),
                                    count_sb[0:1, 0:NBLK].unsqueeze(2).to_broadcast([1, NBLK, NE]), ALU.is_le))
            chain(dve.tensor_reduce(b_exp_f[:], b_past[:], AX.X, ALU.add))
            dve.tensor_scalar(b_exp[:], b_exp_f[:], float(NE - 1), None, ALU.min).then_inc(s_be, 1)

            with dve.Fori(0, NCH) as n:
                for s in range(NSH):
                    dve.wait_ge(s_si, n * NSH + s + 1)
                    dve.wait_ge(s_dn, n * NSH + s + 1)
                    dve.tensor_tensor(act_t[:, s % 2], silu[:, s % 2], ps[2 + s % 2][:], ALU.mult).then_inc(s_ac, 1)
                dve.wait_ge(s_dn, n * NSH + NSH + 2)
                dve.tensor_tensor(x_all[:, bass.ds(n * TC, TC)], ps[6][:].rearrange("p (t e) -> p t e", e=E),
                                  x_all[:, bass.ds(n * TC, TC)], ALU.add).then_inc(s_sa, 1)

            def block_act(m, par):
                dve.wait_ge(s_bs, m + 1)
                dve.wait_ge(s_bu, m + 1)
                dve.tensor_tensor(b_act[:, par], b_silu[:, par], ps[3 + par][:], ALU.mult).then_inc(s_ba, 1)

            def block_act_t(m, par):
                dve.wait_ge(s_bp, m + 1)
                dve.tensor_copy(b_act_t[:, par], ps[5 + par][:]).then_inc(s_bc, 1)

            def slot(m, par):
                block_act(m, par)
                if not (isinstance(m, int) and m < 1):
                    block_act_t(m - 1, 1 - par)

            for m in range(2):
                slot(m, m)
            with dve.Fori(1, NBLK // 2) as p:
                for par in range(2):
                    slot(p * 2 + par, par)
            slot(NBLK - 1, 0)
            block_act_t(NBLK - 1, 0)

            dve.wait_ge(s_sa, NCH + 1)
            for n in range(NCH):
                dve.wait_ge(s_yg[n], 16 * TOP * TC)
                for i, s_c in enumerate((s_c1, s_c2)):
                    for t in range(n * TC, n * TC + TC):
                        if i == 1:
                            dve.wait_ge(s_c1, t + 1)
                        dve.scalar_tensor_tensor(x_all[:, t], y_got[:, i, t], top_w[:, t, i:i + 1], x_all[:, t],
                                                 ALU.mult, ALU.add).then_inc(s_c, 1)

        @block.tensor
        def _(pe):
            pe.wait_ge(s_w, 16 * 11)

            def turn(b, half):
                n = b * 2 + half
                pe.wait_ge(s_xn, n + 1)
                for t in range(TC):
                    ins = pe.transpose(ps[0][:, t * P:t * P + P], xn[:, half, t * P:t * P + P], ident[:])
                ins.then_inc(s_xtp, 1)

            def project(b, half, last):
                n = b * 2 + half
                pe.wait_ge(s_xt, n + 1)
                pe.wait_ge(s_rm[0], n + 1)
                pe.matmul(ps[1][:], wq_p, xn_t[:, half], start=True, stop=True)
                pe.matmul(ps[2][:], wq_s, xn_t[:, half], start=True, stop=True).then_inc(s_qp, 1)
                if not last:
                    turn(b + (half + 1) // 2, (half + 1) % 2)
                pe.wait_ge(s_rm[1], n + 1)
                pe.matmul(ps[4][:], wk_p, xn_t[:, half], start=True, stop=True)
                pe.matmul(ps[5][:], wk_s, xn_t[:, half], start=True, stop=True).then_inc(s_kp, 1)
                pe.wait_ge(s_vr, n + 1)
                for t in range(TC):
                    ins = pe.matmul(ps[6][:, t * P:t * P + P], xn_t[:, half, t * P:t * P + P], wv_sb,
                                    start=True, stop=True)
                ins.then_inc(s_vp, 1)

            pe.transpose(ps[3][0:L, 0:E], wdn_sb, ident[:]).then_inc(s_wdp, 1)
            pe.wait_ge(s_wdc, 1)
            pe.matmul(ps[4][:, 0:E], wdn_t[0:L], wk_up_sb[0:L], start=True, stop=True)
            pe.matmul(ps[4][:, E:2 * E], wdn_t[0:L], wv_up_sb[0:L], start=True, stop=True).then_inc(s_wdp, 1)
            pe.wait_ge(s_wdc, 3)
            pe.wait_ge(s_wp, 18)
            turn(0, 0)
            with pe.Fori(0, B - 1) as b:
                for half in range(2):
                    project(b, half, False)
            for half in range(2):
                project(B - 1, half, half == 1)

            def max_score(i, k, n, ck, qt, heads):
                w = max_width(ck, qt)
                if not (isinstance(i, int) and i == 0 and n < 2):
                    pe.wait_ge(s_rd, i * NU + n - 1)
                for a, j in enumerate(heads):
                    ins = pe.matmul(ps[3 + n % 2][:, a * w:a * w + w], q_op[k][0:MAX_ROW, j, qt * P:qt * P + P],
                                    k_op[k][0:MAX_ROW, j, ck * W:ck * W + w], start=True, stop=True)
                ins.then_inc(s_s1, 1)

            def score(i, k, r, u):
                c, kt = ROUNDS[r]
                lo = low(c, kt)
                w, n = W - lo, CUM[r] + u
                if not (isinstance(i, int) and i == 0 and n < 3):
                    pe.wait_ge(s_ex, i * NU + n - 2)
                for a, j in enumerate(UNITS[r][u]):
                    ins = pe.matmul(ps[(NU * k + n) % 3][:, a * w:a * w + w],
                                    k_op[k][0:ROWS, j, kt * P:kt * P + P],
                                    q_op[k][0:ROWS, j, c * W + lo:c * W + W], start=True, stop=True)
                ins.then_inc(s_s2, 1)

            def add_values(i, k, r):
                c, kt = ROUNDS[r]
                lo = low(c, kt)
                pe.wait_ge(s_ex, i * NU + CUM[r + 1])
                if r == 0:
                    pe.wait_ge(s_vb, i + 1)
                for j in range(HG):
                    ins = pe.matmul(ps[5 + c][32 * j:32 * j + D + 1, lo:W],
                                    v_buf[:, k, kt, j * (D + 1):(j + 1) * (D + 1)], prob[:, r % 3, j, 0:W - lo],
                                    start=(kt == 0), stop=(kt == TC * (c + 1) - 1))
                ins.then_inc(s_pv, 1)

            def turn_max(i, c):
                if c == 0:
                    pe.wait_ge(s_rd, i * NU + MAX_BEFORE[3])
                    src = mx[:, 0].rearrange("p j t -> p (j t)")
                else:
                    pe.wait_ge(s_m1, i + 1)
                    src = mx1[:].rearrange("p j t -> p (j t)")
                pe.transpose(ps[7][0:HG * TC, 0:P], src, ident[:]).then_inc(s_trn, 1)

            def turn_out(c):
                for t in range(TC):
                    ins = pe.transpose(ps[7][:, t * P:t * P + P], o_sb[:, c, t * P:t * P + P], ident[:])
                ins.then_inc(s_trn, 1)

            pe.wait_ge(s_r1[0], NCH + 1)
            pe.wait_ge(s_r1[1], NCH + 1)
            pe.wait_ge(s_vr, NCH + 1)
            pe.wait_ge(s_pc[0], 32)
            pe.wait_ge(s_ld[0], 16 * N_LD)
            for slot in range(NR):
                for n, ck, qt, heads in MAX_UNITS[slot]:
                    max_score(0, 0, n, ck, qt, heads)
            turn_max(0, 0)
            pe.wait_ge(s_mn, 1)
            turn_max(0, 1)
            pe.sem_inc(s_pv, 3)
            pe.wait_ge(s_z, 4)
            pe.wait_ge(s_mr[0], 16)
            for u in range(len(UNITS[0])):
                score(0, 0, 0, u)

            def group(i, k, last, laps):
                nk = (k + 1) % 3
                for r in range(NR):
                    if r == 0 and not last:
                        pe.wait_ge(s_pc[nk], 32)
                        pe.wait_ge(s_ld[nk], laps * (16 * N_LD))
                    si, sk, sr = (i, k, r + 1) if r + 1 < NR else (i + 1, nk, 0)
                    n2 = 0 if (r + 1 == NR and last) else len(UNITS[sr])
                    if n2 and sr in (0, TC):
                        pe.wait_ge(s_mr[0 if sr == 0 else 1], (si + 1) * 16)
                    mine = [] if last else MAX_UNITS[r]
                    most = max(n2, len(mine))
                    for u in range(most):
                        if u == (most + 1) // 2:
                            add_values(i, k, r)
                        if u < n2:
                            score(si, sk, sr, u)
                        if u < len(mine):
                            max_score(i + 1, nk, *mine[u])
                    if most < 2:
                        add_values(i, k, r)
                    if r == OT1_SLOT:
                        pe.wait_ge(s_ob[1], i + 1)
                        pe.wait_ge(s_mn, i * 2 + 2)
                        turn_out(1)
                    if r == OT0_SLOT:
                        pe.wait_ge(s_ob[0], i + 1)
                        pe.wait_ge(s_on, i * 2 + 2)
                        turn_out(0)
                    if r == MT0_SLOT and not last:
                        pe.wait_ge(s_on, i * 2 + 3)
                        turn_max(i + 1, 0)
                    if r == MT1_SLOT and not last:
                        pe.wait_ge(s_mn, i * 2 + 3)
                        turn_max(i + 1, 1)

            with pe.Fori(0, (NG - 1) // 3) as p:
                for k in range(3):
                    group(p * 3 + k, k, False, p + (1 if k < 2 else 2))
            group(NG - 1, 0, True, 0)
            pe.wait_ge(s_ob[1], NG + 1)
            pe.wait_ge(s_on, 2 * NG + 1)
            turn_out(1)

            pe.wait_ge(s_on, 2 * NG + 2)
            pe.transpose(ps[3][:, 0:NE], gw_row[:], ident[0:NE, 0:NE]).then_inc(s_gt, 1)
            pe.wait_ge(s_gc, 1)
            pe.sem_inc(s_atp, 2)

            def project_out(b, half):
                n = b * 2 + half
                pe.wait_ge(s_att, n + 1)
                pe.wait_ge(s_x1, n + 1)
                for t in range(TC):
                    ins = pe.matmul(ps[1 + 3 * half][:, t * P:t * P + P], a_t[:, half, t * P:t * P + P], wo_sb[:],
                                    start=True, stop=True)
                ins.then_inc(s_y, 1)

            def turn_attn(b, half):
                n = b * 2 + half
                pe.wait_ge(s_at, n + 1)
                for t in range(TC):
                    ins = pe.transpose(ps[5 * half][:, t * P:t * P + P], a_tok[:, half, t * P:t * P + P], ident[:])
                ins.then_inc(s_atp, 1)

            turn_attn(0, 0)
            with pe.Fori(0, B - 1) as b:
                for half in range(2):
                    turn_attn(b + half, 1 - half)
                    project_out(b, half)
            turn_attn(B - 1, 1)
            project_out(B - 1, 0)
            project_out(B - 1, 1)

            def turn_x(b, half):
                n = b * 2 + half
                pe.wait_ge(s_xn2, n + 1)
                for t in range(TC):
                    ins = pe.transpose(ps[2 + 4 * half][:, t * P:t * P + P], xn2[:, half, t * P:t * P + P], ident[:])
                ins.then_inc(s_xp2, 1)

            def route(b, half):
                n = b * 2 + half
                pe.wait_ge(s_xc2, n + 1)
                pe.wait_ge(s_xk2, n + 1)
                if half == 0:
                    pe.wait_ge(s_lc, b + 1)
                for t in range(TC):
                    a = (half * TC + t) * NE
                    ins = pe.matmul(ps[3][:, a:a + NE], xn2_c[:, half, t * P:t * P + P], gw_t[:],
                                    start=True, stop=True)
                ins.then_inc(s_lg, 1)

            turn_x(0, 0)
            with pe.Fori(0, B - 1) as b:
                for half in range(2):
                    turn_x(b + half, 1 - half)
                    route(b, half)
            turn_x(B - 1, 1)
            route(B - 1, 0)
            route(B - 1, 1)

            pe.wait_ge(s_z, 4)
            pe.wait_ge(s_pk, 1)
            rows = picked[:].rearrange("p t e -> p (t e)")
            pe.matmul(ps[4][:, 0:NT * NE], before_sb[:], rows, start=True, stop=True)
            pe.matmul(ps[5][:, 0:NT * NE], ones_sb[:], rows, start=True, stop=True).then_inc(s_cn, 1)

            pe.wait_ge(s_ew, 16 * (2 + NE + 3))
            pe.wait_ge(s_lc, B + 1)
            pe.sem_inc(s_dn, 2)
            with pe.Fori(0, NCH) as n:
                def down(s):
                    pe.wait_ge(s_ac, n * NSH + s + 3)
                    if s == 0:
                        pe.wait_ge(s_sa, n + 1)
                    for t in range(TC):
                        ins = pe.matmul(ps[6][:, t * P:t * P + P], act_t[:, s % 2, t * P:t * P + P], sd_sb[:, s],
                                        start=(s == 0 and t == 0), stop=(s == NSH - 1 and t == TC - 1),
                                        skip_group_check=True)
                    ins.then_inc(s_dn, 1)

                for s in range(NSH):
                    pe.wait_ge(s_ac, n * NSH + s + 1)
                    for w, bank in ((sg_sb, 0), (su_sb, 2)):
                        ins = pe.matmul(ps[bank + s % 2][:], w[:, s * P:s * P + P], xn2_t[:, n], start=True, stop=True)
                    ins.then_inc(s_h, 1)
                for s in range(NSH):
                    down(s)

            def expert(m):
                return pe.value_load(b_exp[0:1, bass.ds(m, 1)], min_val=0, max_val=NE - 1)

            def block_turn(m, par, lap):
                pe.wait_ge(s_bl[par], lap * 16 + 16)
                if not (isinstance(m, int) and m < 1):
                    pe.wait_ge(s_bt, m)
                pe.transpose(ps[0][:, 0:P], xb[:, par], ident[:]).then_inc(s_bx, 1)

            def block_hidden(m, par):
                e = expert(m)
                pe.wait_ge(s_bt, m + 1)
                if not (isinstance(m, int) and m < 2):
                    pe.wait_ge(s_ba, m - 1)
                pe.matmul(ps[1 + par][:], xb_t[:, par], wg_sb[:, e], start=True, stop=True).then_inc(s_bg, 1)
                pe.matmul(ps[3 + par][:], xb_t[:, par], wu_sb[:, e], start=True, stop=True).then_inc(s_bu, 1)

            def block_act_turn(m, par):
                pe.wait_ge(s_ba, m + 1)
                for c in range(F // P):
                    ins = pe.transpose(ps[5 + par][:, c * P:c * P + P], b_act[:, par, c * P:c * P + P], ident[:])
                ins.then_inc(s_bp, 1)

            def block_down(m, par):
                e = expert(m)
                pe.wait_ge(s_bc, m + 1)
                pe.wait_ge(s_by, m + 1)
                for c in range(F // P):
                    ins = pe.matmul(ps[7][:, 0:E], b_act_t[:, par, c * P:c * P + P], wd_sb[:, e, c],
                                    start=(c == 0), stop=(c == F // P - 1))
                ins.then_inc(s_bd, 1)

            def slot(m, par, lap):
                block_hidden(m, par)
                if not (isinstance(m, int) and m + 1 >= NBLK):
                    block_turn(m + 1, 1 - par, lap + par)
                if not (isinstance(m, int) and m < 2):
                    block_down(m - 2, par)
                if not (isinstance(m, int) and m < 1):
                    block_act_turn(m - 1, 1 - par)

            pe.wait_ge(s_sa, NCH + 1)
            pe.wait_ge(s_be, 1)
            block_turn(0, 0, 0)
            for m in range(2):
                slot(m, m, 0)
            with pe.Fori(1, NBLK // 2) as p:
                for par in range(2):
                    slot(p * 2 + par, par, p)
            slot(NBLK - 1, 0, NBLK // 2)
            block_down(NBLK - 2, 1)
            block_act_turn(NBLK - 1, 0)
            block_down(NBLK - 1, 0)


_INS = ['L0_attn_x', 'L0_attn_wq', 'L0_attn_w_down', 'L0_attn_wk_up', 'L0_attn_wv_up', 'L0_attn_wo',
        'L0_ffn_gate_w', 'L0_ffn_gate_k', 'L0_ffn_up_k', 'L0_ffn_down_k', 'L0_ffn_sh_gate', 'L0_ffn_sh_up',
        'L0_ffn_sh_down']


def shape_tables():
    inv = 1.0 / 10000.0 ** (np.arange(0, D, 2, dtype=np.float32) / D)
    ang = np.outer(np.arange(T, dtype=np.float32), inv)
    cos, sin = np.cos(ang).astype(np.float32), np.sin(ang).astype(np.float32)
    d = (np.arange(P) // HG) % D
    cos_t = cos[:, d // 2].T
    sin_t = sin[:, d // 2].T * np.where(d % 2 == 0, -1.0, 1.0).astype(np.float32)[:, None]
    page = np.arange(T) // PAGE
    rows = np.arange(NPAGE)[:, None]
    page_k = np.concatenate([page[None, :] == rows, np.ones((3, T))])
    page_q = np.where(page[None, :] < rows, NEG, 0.0)
    return {
        "cos_t": np.ascontiguousarray(cos_t, np.float32),
        "sin_t": np.ascontiguousarray(sin_t, np.float32),
        "page_k": (page_k.astype(np.float32).view(np.uint32) >> 16).astype(np.uint16),
        "page_q": (page_q.astype(np.float32).view(np.uint32) >> 16).astype(np.uint16),
        "eye": np.eye(P, dtype=np.float32),
        "before": np.triu(np.ones((P, P), np.float32), 1),
        "count_t": np.tile(np.concatenate([np.arange(NBLK), P * np.arange(MAXB)]).astype(np.float32), (P, 1)),
    }


def kernel(**inputs):
    import concourse.bacc as _bacc
    from concourse.bass_utils import run_bass_kernel_spmd as _run

    nc = _bacc.Bacc("TRN2", target_bir_lowering=False, num_devices=1)
    arrays, args = {}, []
    given = [(n, np.ascontiguousarray(inputs[n])) for n in _INS] + list(shape_tables().items())
    for name, a in given:
        arrays[f"in_{name}_dram"] = a
        args.append(nc.dram_tensor(f"in_{name}_dram", a.shape, mybir.dt.from_np(a.dtype), kind="ExternalInput").ap())
    out = nc.dram_tensor("out_0_dram", (B, T, E), F32, kind="ExternalOutput").ap()
    build(nc, *args, out)
    r = _run(nc, [arrays], core_ids=[0])
    return r.results[0]["out_0_dram"]
```
